# Optimizing a Trainium2 kernel written in Bass

```python
import numpy as np
import jax
import jax.numpy as jnp

def _softmax(x, axis=-1):
    return jax.nn.softmax(x, axis=axis)
def _gelu(x):
    return jax.nn.gelu(x, approximate=True)
def _silu(x):
    return jax.nn.silu(x)
def _sigmoid(x):
    return jax.nn.sigmoid(x)
def _layernorm(x, axis=-1, eps=1e-5):
    m = jnp.mean(x, axis=axis, keepdims=True)
    v = jnp.var(x, axis=axis, keepdims=True)
    return (x - m) / jnp.sqrt(v + eps)
def _scatter_add(tgt, idx, src, axis=0):
    return tgt.at[idx].add(src)
def _segment_sum(src, seg, n):
    return jax.ops.segment_sum(src, seg, n)

kernel_name = 'mk_conv_seq_d2_conv_nhwc256_e622e6'

def setup_inputs(seed: int = 0):
    np.random.seed(seed)
    _w = jnp.asarray
    def _rec_inputs():
        import jax
        import jax.numpy as jnp
        _gk = jax.random.key(seed)
        x = -0.0003929 + 0.9999 * jax.random.normal(jax.random.fold_in(_gk, 1), (16, 64, 64, 256), jnp.float32)
        return x
    x = _rec_inputs()
    def _L0_conv_setup():
        import jax, jax.numpy as jnp
        import numpy as np

        def _maxpool2x2(x):
            B, H, W, C = x.shape
            x = x.reshape(B, H // 2, 2, W // 2, 2, C)
            return x.max(axis=(2, 4))
        key = jax.random.key(seed)
        ks = jax.random.split(key, 5)
        B, H, W, C = (16, 64, 64, 256)
        Ca, Cg = (C // 8, C // 2)
        sc = 0.05
        return {'x': jax.random.normal(ks[0], (B, H, W, C), dtype=jnp.float32), 'w_theta': jax.random.normal(ks[1], (C, Ca), dtype=jnp.float32) * sc, 'w_phi': jax.random.normal(ks[2], (C, Ca), dtype=jnp.float32) * sc, 'w_g': jax.random.normal(ks[3], (C, Cg), dtype=jnp.float32) * sc, 'w_out': jax.random.normal(ks[4], (Cg, C), dtype=jnp.float32) * sc, 'sigma': jnp.float32(1.0)}
    _L0_conv_all = _L0_conv_setup()
    _L0_conv_in = {k: v for k, v in _L0_conv_all.items() if k in ('w_theta', 'w_phi', 'w_g', 'w_out', 'sigma', )}
    del _L0_conv_all

    def _L1_conv_setup():
        import jax, jax.numpy as jnp
        import numpy as np
        from jax.scipy.linalg import cholesky, solve_triangular
        EPS = 0.001
        key = jax.random.key(seed)
        k1, = jax.random.split(key, 1)
        b, w, h, c = (64, 56, 56, 256)
        x = jax.random.normal(k1, (b, w, h, c), dtype=jnp.float32)
        gamma = jnp.ones((c,), dtype=jnp.float32)
        beta = jnp.zeros((c,), dtype=jnp.float32)
        return {'x': x, 'gamma': gamma, 'beta': beta}
    _L1_conv_all = _L1_conv_setup()
    _L1_conv_in = {k: v for k, v in _L1_conv_all.items() if k in ('gamma', 'beta', )}
    del _L1_conv_all

    return {
        "x": x,
        "L0_conv_w_theta": _L0_conv_in["w_theta"],
        "L0_conv_w_phi": _L0_conv_in["w_phi"],
        "L0_conv_w_g": _L0_conv_in["w_g"],
        "L0_conv_w_out": _L0_conv_in["w_out"],
        "L0_conv_sigma": _L0_conv_in["sigma"],
        "L1_conv_gamma": _L1_conv_in["gamma"],
        "L1_conv_beta": _L1_conv_in["beta"],
    }

def reference(x, L0_conv_w_theta, L0_conv_w_phi, L0_conv_w_g, L0_conv_w_out, L0_conv_sigma, L1_conv_gamma, L1_conv_beta):
    import jax
    import jax.numpy as jnp
    def _L0_conv_ref(x, w_theta, w_phi, w_g, w_out, sigma):
        import jax, jax.numpy as jnp
        import numpy as np

        def _maxpool2x2(x):
            B, H, W, C = x.shape
            x = x.reshape(B, H // 2, 2, W // 2, 2, C)
            return x.max(axis=(2, 4))
        B, H, W, C = x.shape
        theta = jnp.einsum('bhwc,cd->bhwd', x, w_theta).reshape(B, H * W, -1)
        phi = _maxpool2x2(jnp.einsum('bhwc,cd->bhwd', x, w_phi))
        phi = phi.reshape(B, H // 2 * (W // 2), -1)
        attn = jax.nn.softmax(jnp.einsum('bnd,bmd->bnm', theta, phi), axis=-1)
        g = _maxpool2x2(jnp.einsum('bhwc,cd->bhwd', x, w_g))
        g = g.reshape(B, H // 2 * (W // 2), -1)
        attn_g = jnp.einsum('bnm,bmd->bnd', attn, g).reshape(B, H, W, -1)
        attn_g = jnp.einsum('bhwd,dc->bhwc', attn_g, w_out)
        return sigma * attn_g + x

    def _L1_conv_ref(x, gamma, beta):
        import jax, jax.numpy as jnp
        import numpy as np
        from jax.scipy.linalg import cholesky, solve_triangular
        EPS = 0.001
        b, w, h, c = x.shape
        n = b * w * h
        x_flat = jnp.transpose(x, (3, 0, 1, 2)).reshape(c, n)
        m = jnp.mean(x_flat, axis=1, keepdims=True)
        f = x_flat - m
        ff = f @ f.T / (jnp.float32(n) - 1.0)
        ff = (1.0 - EPS) * ff + EPS * jnp.eye(c, dtype=x.dtype)
        L = cholesky(ff, lower=True)
        inv_sqrt = solve_triangular(L, jnp.eye(c, dtype=x.dtype), lower=True)
        f_hat = inv_sqrt @ f
        out = jnp.transpose(f_hat.reshape(c, b, w, h), (1, 2, 3, 0))
        out = out * gamma.reshape(1, 1, 1, c) + beta.reshape(1, 1, 1, c)
        return out

    def _gn(v, G=32, eps=1e-5):
        B_, H_, W_, C_ = v.shape
        g = v.reshape(B_, H_, W_, G, C_ // G)
        m = jnp.mean(g, axis=(1, 2, 4), keepdims=True)
        s = jnp.var(g, axis=(1, 2, 4), keepdims=True)
        return ((g - m) / jnp.sqrt(s + eps)).reshape(v.shape)

    def _ln_c(v, eps=1e-6):
        m = jnp.mean(v, axis=-1, keepdims=True)
        s = jnp.var(v, axis=-1, keepdims=True)
        return (v - m) / jnp.sqrt(s + eps)

    def _ln_t(v, eps=1e-5):
        m = jnp.mean(v, axis=-1, keepdims=True)
        s = jnp.var(v, axis=-1, keepdims=True)
        return (v - m) / jnp.sqrt(s + eps)

    def _to_tokens(v):
        B_, H_, W_, C_ = v.shape
        return v.reshape(B_, H_ * W_, C_)
    def _from_tokens(t, like):
        return t.reshape(like.shape)

    x = _L0_conv_ref(x, L0_conv_w_theta, L0_conv_w_phi, L0_conv_w_g, L0_conv_w_out, L0_conv_sigma)
    x = _L1_conv_ref(x, L1_conv_gamma, L1_conv_beta)
    return x


_drawn_inputs = setup_inputs


def setup_inputs(seed=0):
    import zlib

    import numpy as np

    out = dict(_drawn_inputs(seed))
    spreads = {'L1_conv_gamma': (1.0, 0.2), 'L1_conv_beta': (0.0, 0.1)}
    factors = {}
    for name, (base, spread) in spreads.items():
        noise = np.random.default_rng([zlib.crc32(name.encode()), seed]).standard_normal(out[name].shape)
        drawn = base * np.exp(spread * noise) if base else spread * noise
        out[name] = jnp.asarray(drawn.astype(out[name].dtype))
    for name, factor in factors.items():
        out[name] = (out[name] * factor).astype(out[name].dtype)
    return out
```

```python
from contextlib import ExitStack

import concourse.bass as bass
from concourse import mybir

F32 = mybir.dt.float32
F32R = mybir.dt.float32r
ALU = mybir.AluOpType
ACT = mybir.ActivationFunctionType
AX = mybir.AxisListType

P = 128
NT = 512
NC = NT // P
WHITEN_EPS = 1e-3


def attention_whitening_kernel(nc, xT, xN, w_theta, w_phi, w_g, w_out, sigma, gamma, beta, outT):
    B, C, N = xT.shape
    DA = w_theta.shape[1]
    DG = w_g.shape[1]
    CC = C // P
    TILES = N // NT
    WIDTH = 64
    ROWS = NT // WIDTH
    M = N // 4
    MB = M // P
    assert MB == TILES and DG == P and 3 * DA + DA == P
    TOTAL = B * N
    SHIFT = 3 * DA
    LAST = TILES * MB
    CHUNKS = TILES * NC
    RING = 4
    SETUP_LOADS = 7 * CC + 2

    yN = nc.dram_tensor("y_spill", [B * TILES, NC, P, C], F32, kind="Internal").ap()

    with ExitStack() as ctx:
        def sb(name, shape, dt=F32):
            return ctx.enter_context(nc.sbuf_tensor(name, shape, dt))

        def ps(name, shape):
            return ctx.enter_context(nc.psum_tensor(name, shape, F32))

        def sem(name):
            return ctx.enter_context(nc.semaphore(name))

        ps_scores = ps("ps_scores", [P, 2 * NT])
        ps_st = ps("ps_st", [P, 2, NT])
        ps_o = ps("ps_o", [P, NT])
        ps_y = ps("ps_y", [P, 2, C])
        ps_cov = ps("ps_cov", [P, 2, NT])

        w_tp = sb("w_tp", [P, CC, P])
        w_tp_hi = sb("w_tp_hi", [P, CC, P], F32R)
        w_tp_lo = sb("w_tp_lo", [P, CC, P], F32R)
        w_gs = sb("w_gs", [P, CC, DG])
        w_g_hi = sb("w_g_hi", [P, CC, DG], F32R)
        w_g_lo = sb("w_g_lo", [P, CC, DG], F32R)
        w_o = sb("w_o", [P, C])
        w_o_hi = sb("w_o_hi", [P, C], F32R)
        w_o_lo = sb("w_o_lo", [P, C], F32R)
        sig = sb("sig", [P, 1])
        gam = sb("gam", [P, CC])
        bet = sb("bet", [P, CC])
        ident = sb("ident", [P, P])
        ident_r = sb("ident_r", [P, P], F32R)
        ones = sb("ones", [P, P])
        below = sb("below", [P, P])
        zeros_r = sb("zeros_r", [P, NT], F32R)

        x_raw = sb("x_raw", [P, 2, CC, NT])
        x_hi = sb("x_hi", [P, 2, CC, NT], F32R)
        x_lo = sb("x_lo", [P, 2, CC, NT], F32R)
        theta = sb("theta", [P, N], F32R)
        phi = sb("phi", [P, M], F32R)
        phi_pool = sb("phi_pool", [P, 2, P])
        phi_hi = sb("phi_hi", [P, 2, P], F32R)
        g_pool = sb("g_pool", [P, 2, P])
        g_hi = sb("g_hi", [P, MB, DG], F32R)
        g_lo = sb("g_lo", [P, MB, DG], F32R)
        neg_max = sb("neg_max", [P, RING, NC], F32R)
        total = sb("total", [P, RING, NC])
        scale = sb("scale", [P, 2, NC])
        recip = sb("recip", [P, 2, NC])
        dump = sb("dump", [P, 2, M])
        e_val = sb("e_val", [P, RING, NT])
        e_hi = sb("e_hi", [P, RING, NT], F32R)
        e_lo = sb("e_lo", [P, RING, NT], F32R)
        o_hi = sb("o_hi", [P, 2, NT], F32R)
        o_lo = sb("o_lo", [P, 2, NT], F32R)
        x_nat = sb("x_nat", [P, 3, NC, C])
        y_val = sb("y_val", [P, 3, NC, C])
        y_split = sb("y_split", [P, 2, NC, 2 * C], F32R)
        y_sum = sb("y_sum", [P, NC, C])

        s_setup_dma = sem("s_setup_dma")
        s_const0 = sem("s_const0")
        s_const = sem("s_const")
        s_whi = sem("s_whi")
        s_wlo = sem("s_wlo")
        s_cov_open = sem("s_cov_open")
        cleared = []

        def isem(name):
            s = sem(name)
            cleared.append(s)
            return s

        s_xt = [isem("s_xt0"), isem("s_xt1")]
        s_xhi = isem("s_xhi")
        s_xlo_v = isem("s_xlo_v")
        s_xlo_p = isem("s_xlo_p")
        s_tp = isem("s_tp")
        s_g = isem("s_g")
        s_th_hi = isem("s_th_hi")
        s_th_lo = isem("s_th_lo")
        s_phipool = isem("s_phipool")
        s_gpool = isem("s_gpool")
        s_gT = isem("s_gT")
        s_ghi = isem("s_ghi")
        s_glo = isem("s_glo")
        s_phihi = isem("s_phihi")
        s_phi = isem("s_phi")
        s_philo = isem("s_philo")
        s_scores = isem("s_scores")
        s_max = isem("s_max")
        s_z = isem("s_z")
        s_rowT = isem("s_rowT")
        s_row = isem("s_row")
        s_st = isem("s_st")
        s_e = isem("s_e")
        s_ehi = isem("s_ehi")
        s_elo_v = isem("s_elo_v")
        s_elo_p = isem("s_elo_p")
        s_av = isem("s_av")
        s_ohi = isem("s_ohi")
        s_olo = isem("s_olo")
        s_yps = isem("s_yps")
        s_recip = isem("s_recip")
        s_scale = isem("s_scale")
        s_y = isem("s_y")
        s_yhi = isem("s_yhi")
        s_ylo = isem("s_ylo")
        s_ysum = isem("s_ysum")
        s_cov = isem("s_cov")
        s_xn = [isem(f"s_xn{k}") for k in range(3)]
        s_yst = [isem(f"s_yst{k}") for k in range(3)]

        with nc.Block() as block:
            @block.sync
            def _(sp):
                for cc in range(CC):
                    rows = slice(cc * P, (cc + 1) * P)
                    for k in range(3):
                        sp.dma_start(w_tp[:, cc, k * DA:(k + 1) * DA], w_theta[rows, :]).then_inc(s_setup_dma, 16)
                    sp.dma_start(w_tp[:, cc, 3 * DA:], w_phi[rows, :]).then_inc(s_setup_dma, 16)
                    sp.dma_start(w_gs[:, cc, :], w_g[rows, :]).then_inc(s_setup_dma, 16)
                sp.dma_start(w_o[:, :], w_out).then_inc(s_setup_dma, 16)
                sp.dma_start(sig[:, :], sigma.partition_broadcast(P)).then_inc(s_setup_dma, 16)
                for a in range(CC):
                    for dst, src in ((gam, gamma), (bet, beta)):
                        sp.dma_start(dst[:, a:a + 1],
                                     src[a * P:(a + 1) * P].rearrange("(p o) -> p o", o=1)).then_inc(s_setup_dma, 16)
                sp.wait_ge(s_setup_dma, 16 * SETUP_LOADS)

            @block.gpsimd
            def _(pool):
                pool.memset(ident[:, :], 0.0).then_inc(s_const0, 1)
                pool.memset(below[:, :], 0.0).then_inc(s_const0, 1)
                pool.memset(ones[:, :], 1.0).then_inc(s_const, 1)
                pool.memset(y_sum[:, :, :], 0.0).then_inc(s_const, 1)
                pool.wait_ge(s_const0, 2)
                pool.affine_select(out=ident[:, :], in_=ident[:, :], compare_op=ALU.not_equal, fill=1.0,
                                   base=0, pattern=[[-1, P]], channel_multiplier=1).then_inc(s_const, 1)
                pool.affine_select(out=below[:, :], in_=below[:, :], compare_op=ALU.is_ge, fill=-1.0,
                                   base=0, pattern=[[1, P]], channel_multiplier=-1).then_inc(s_const, 1)

            @block.vector
            def _(dve):
                dve.memset(zeros_r[:, :].bitcast(F32), 0.0).then_inc(s_const, 1)
                dve.wait_ge(s_const, 5)
                dve.tensor_copy(ident_r[:, :], ident[:, :]).then_inc(s_const, 1)
                dve.tensor_copy(phi[SHIFT:SHIFT + 1, :],
                                ones[SHIFT:SHIFT + 1, 0:1].to_broadcast([1, M])).then_inc(s_const, 1)
                dve.wait_ge(s_setup_dma, 16 * SETUP_LOADS)
                pairs = ((w_tp, w_tp_hi, w_tp_lo), (w_gs, w_g_hi, w_g_lo), (w_o, w_o_hi, w_o_lo))
                for raw, hi, _lo in pairs:
                    dve.tensor_copy(hi[:], raw[:]).then_inc(s_whi, 1)
                for k, (raw, hi, lo) in enumerate(pairs):
                    dve.wait_ge(s_whi, k + 1)
                    dve.tensor_tensor(lo[:], raw[:], hi[:].bitcast(F32), ALU.subtract).then_inc(s_wlo, 1)

            @block.tensor
            def _(pe):
                pe.wait_ge(s_const, 5)
                for a in range(2):
                    pe.matmul(ps_cov[:, a, :], zeros_r[:, 0:P], zeros_r[:, :], start=True, stop=False,
                              skip_group_check=True).then_inc(s_cov_open, 1)

        def pool_takes(q):
            return q % 4 == 3

        def dve_splits(q):
            return sum(not pool_takes(k) for k in range(q))

        def pool_splits(q):
            return sum(pool_takes(k) for k in range(q))

        with nc.Fori(0, B) as img:
            with nc.Block() as block:
                @block.sync
                def _(sp):
                    def load_xt(t):
                        if t >= 2:
                            sp.wait_ge(s_xhi, t - 1)
                            sp.wait_ge(s_xlo_v, t - 1)
                            sp.wait_ge(s_xlo_p, t - 1)
                        sp.dma_start(x_raw[:, t % 2, :, :],
                                     xT[img, :, t * NT:(t + 1) * NT].rearrange("(a p) n -> p a n", p=P)
                                     ).then_inc(s_xt[t % 2], 16)

                    def load_xn(t):
                        if t >= 3:
                            sp.wait_ge(s_y, 2 * (t - 2))
                        sp.dma_start(x_nat[:, t % 3, :, :],
                                     xN[img * TILES + t].rearrange("j p c -> p j c")).then_inc(s_xn[t % 3], 16)

                    def store_y(t):
                        sp.wait_ge(s_y, 2 * (t + 1))
                        sp.dma_start(yN[img * TILES + t].rearrange("j p c -> p j c"),
                                     y_val[:, t % 3, :, :]).then_inc(s_yst[t % 3], 16)

                    for t in range(TILES):
                        load_xt(t)
                    for t in range(3):
                        load_xn(t)
                    for t in range(TILES):
                        store_y(t)
                        if t + 3 < TILES:
                            load_xn(t + 3)
                    for k in range(3):
                        sp.wait_ge(s_yst[k], 16 * len(range(k, TILES, 3)))

                @block.tensor
                def _(pe):
                    def project(t):
                        slot = t % 2
                        acc = ps_scores[:, slot * NT:(slot + 1) * NT]
                        pe.wait_ge(s_xhi, t + 1)
                        if t >= 2:
                            pe.wait_ge(s_th_lo, t - 1)
                        for cc in range(CC):
                            pe.matmul(acc, w_tp_hi[:, cc, :], x_hi[:, slot, cc, :], start=(cc == 0), stop=False)
                            pe.matmul(acc, w_tp_lo[:, cc, :], x_hi[:, slot, cc, :], start=False, stop=False)
                        pe.wait_ge(s_xlo_v, t + 1)
                        pe.wait_ge(s_xlo_p, t + 1)
                        for cc in range(CC):
                            last = pe.matmul(acc, w_tp_hi[:, cc, :], x_lo[:, slot, cc, :],
                                             start=False, stop=(cc == CC - 1))
                        last.then_inc(s_tp, 1)
                        if t >= 2:
                            pe.wait_ge(s_gpool, t - 1)
                        acc = ps_st[:, slot, :]
                        for cc in range(CC):
                            pe.matmul(acc, w_g_hi[:, cc, :], x_hi[:, slot, cc, :], start=(cc == 0), stop=False)
                            pe.matmul(acc, w_g_lo[:, cc, :], x_hi[:, slot, cc, :], start=False, stop=False)
                            last = pe.matmul(acc, w_g_hi[:, cc, :], x_lo[:, slot, cc, :],
                                             start=False, stop=(cc == CC - 1))
                        last.then_inc(s_g, 1)

                    def turn_g(t):
                        bank = ps_o[:, 0:P] if t % 2 == 0 else ps_y[:, 0, 0:P]
                        pe.wait_ge(s_gpool, t + 1)
                        if t >= 2:
                            pe.wait_ge(s_glo, t - 1)
                        pe.transpose(bank, g_pool[:, t % 2, :], ident[:, :]).then_inc(s_gT, 1)

                    def scores(c):
                        if c >= 1:
                            pe.wait_ge(s_z, c)
                        for h in range(2):
                            last = pe.matmul(ps_scores[:, h * NT:(h + 1) * NT], theta[0:SHIFT, c * P:(c + 1) * P],
                                             phi[0:SHIFT, h * NT:(h + 1) * NT], start=True, stop=True)
                        last.then_inc(s_scores, 1)

                    def turn_max(t):
                        pe.wait_ge(s_max, NC * (t + 1))
                        if t >= 2:
                            pe.wait_ge(s_y, 2 * (t - 1))
                        row = ps_y[0:1, :, :].rearrange("p a c -> p (a c)")
                        for j in range(NC):
                            last = pe.transpose(row[:, j * P:(j + 1) * P].bitcast(F32R),
                                                neg_max[:, t % RING, j:j + 1], ident_r[:, :])
                        last.then_inc(s_rowT, 1)

                    def scores_t(q):
                        t, b = divmod(q, MB)
                        if b == 0:
                            pe.wait_ge(s_row, t + 1)
                        if q >= 2:
                            pe.wait_ge(s_e, q - 1)
                        pe.matmul(ps_st[:, q % 2, :], phi[0:SHIFT + 1, b * P:(b + 1) * P],
                                  theta[0:SHIFT + 1, t * NT:(t + 1) * NT], start=True, stop=True).then_inc(s_st, 1)

                    def attend(q):
                        t, b = divmod(q, MB)
                        if b == 0 and t >= 1:
                            pe.wait_ge(s_olo, t)
                        pe.wait_ge(s_ehi, q + 1)
                        pe.matmul(ps_o[:, :], g_hi[:, b, :], e_hi[:, q % RING, :], start=(b == 0), stop=False)
                        pe.matmul(ps_o[:, :], g_lo[:, b, :], e_hi[:, q % RING, :], start=False, stop=False)
                        if pool_takes(q):
                            pe.wait_ge(s_elo_p, pool_splits(q + 1))
                        else:
                            pe.wait_ge(s_elo_v, dve_splits(q + 1))
                        pe.matmul(ps_o[:, :], g_hi[:, b, :], e_lo[:, q % RING, :],
                                  start=False, stop=(b == MB - 1)).then_inc(s_av, 1)

                    def project_out(t, half):
                        if half == 0:
                            pe.wait_ge(s_olo, t + 1)
                            if t + 2 <= TILES:
                                pe.wait_ge(s_row, min(t + 2, TILES))
                        else:
                            pe.wait_ge(s_y, 2 * t + 1)
                        for k in range(2):
                            cols = slice((2 * half + k) * P, (2 * half + k + 1) * P)
                            pe.matmul(ps_y[:, k, :], o_hi[:, t % 2, cols], w_o_hi[:, :], start=True, stop=False)
                            pe.matmul(ps_y[:, k, :], o_hi[:, t % 2, cols], w_o_lo[:, :], start=False, stop=False)
                            last = pe.matmul(ps_y[:, k, :], o_lo[:, t % 2, cols], w_o_hi[:, :],
                                             start=False, stop=True)
                        last.then_inc(s_yps, 1)

                    def moments(t):
                        pe.wait_ge(s_yhi, t + 1)
                        pe.wait_ge(s_ylo, t + 1)
                        for j in range(NC):
                            y2 = y_split[:, t % 2, j, :]
                            pe.matmul(ps_cov[:, 0, :], y2[:, 0:P], y2, start=False, stop=False,
                                      skip_group_check=True)
                            last = pe.matmul(ps_cov[:, 1, 0:2 * C - P], y2[:, P:2 * P], y2[:, P:],
                                             start=False, stop=False, skip_group_check=True)
                        last.then_inc(s_cov, 1)

                    for t in range(TILES):
                        project(t)
                        if t >= 1:
                            turn_g(t - 1)
                    turn_g(TILES - 1)
                    pe.wait_ge(s_phi, 2 * TILES)
                    pe.wait_ge(s_philo, TILES)
                    pe.wait_ge(s_th_lo, TILES)
                    pe.wait_ge(s_gpool, TILES)
                    pe.wait_ge(s_glo, TILES)
                    for c in range(NC + 2):
                        scores(c)
                    turn_max(0)
                    scores_t(0)
                    scores_t(1)
                    for t in range(TILES):
                        for b in range(MB):
                            q = t * MB + b
                            c = NC * (t + 1) + 2 + b // 2
                            if b % 2 == 0 and c < CHUNKS:
                                scores(c)
                            if b == 5 and t + 1 < TILES:
                                turn_max(t + 1)
                            if q + 2 < LAST:
                                scores_t(q + 2)
                            if b == 0 and t >= 2:
                                moments(t - 2)
                            attend(q)
                            if b in (1, 3) and t >= 1:
                                project_out(t - 1, b // 2)
                    project_out(TILES - 1, 0)
                    project_out(TILES - 1, 1)
                    moments(TILES - 2)
                    moments(TILES - 1)

                @block.scalar
                def _(act):
                    def split_x(t):
                        act.wait_ge(s_xt[t % 2], 16 * (t // 2 + 1))
                        if t >= 2:
                            act.wait_ge(s_g, t - 1)
                        act.copy(x_hi[:, t % 2, :, :], x_raw[:, t % 2, :, :]).then_inc(s_xhi, 1)

                    def theta_hi(t):
                        act.wait_ge(s_tp, t + 1)
                        act.copy(theta[0:SHIFT, t * NT:(t + 1) * NT],
                                 ps_scores[0:SHIFT, (t % 2) * NT:(t % 2 + 1) * NT]).then_inc(s_th_hi, 1)

                    def split_g(t):
                        bank = ps_o[:, 0:P] if t % 2 == 0 else ps_y[:, 0, 0:P]
                        act.wait_ge(s_gT, t + 1)
                        act.copy(g_hi[:, t, :], bank).then_inc(s_ghi, 1)

                    def stack_phi(t):
                        cols = slice(t * P, (t + 1) * P)
                        act.wait_ge(s_phipool, t + 1)
                        if t >= 2:
                            act.wait_ge(s_philo, t - 1)
                        act.copy(phi_hi[SHIFT:, t % 2, :], phi_pool[SHIFT:, t % 2, :]).then_inc(s_phihi, 1)
                        act.wait_ge(s_phihi, t + 1)
                        for k in range(2):
                            act.copy(phi[k * DA:(k + 1) * DA, cols],
                                     phi_hi[SHIFT:, t % 2, :].bitcast(F32)).then_inc(s_phi, 1)

                    def exp_sum(c):
                        t, j = divmod(c, NC)
                        act.wait_ge(s_max, c + 1)
                        if c >= 2:
                            act.wait_ge(s_z, c - 1)
                        act.activation(dump[:, c % 2, :], ps_scores[:, :], ACT.Exp,
                                       bias=neg_max[:, t % RING, j:j + 1].bitcast(F32),
                                       accum_out=total[:, t % RING, j:j + 1]).then_inc(s_z, 1)

                    def copy_row(t):
                        act.wait_ge(s_rowT, t + 1)
                        act.copy(theta[SHIFT:SHIFT + 1, t * NT:(t + 1) * NT],
                                 ps_y[0:1, :, :].rearrange("p a c -> p (a c)")).then_inc(s_row, 1)

                    def exponentiate(q):
                        act.wait_ge(s_st, q + 1)
                        if q >= RING:
                            k = q - RING + 1
                            act.wait_ge(s_elo_v, dve_splits(k))
                            if pool_splits(k):
                                act.wait_ge(s_elo_p, pool_splits(k))
                        act.activation(e_val[:, q % RING, :], ps_st[:, q % 2, :], ACT.Exp).then_inc(s_e, 1)

                    def split_e(q):
                        act.wait_ge(s_e, q + 1)
                        if q >= RING:
                            act.wait_ge(s_av, q - RING + 1)
                        act.copy(e_hi[:, q % RING, :], e_val[:, q % RING, :]).then_inc(s_ehi, 1)

                    def split_o(t):
                        act.wait_ge(s_av, MB * (t + 1))
                        if t >= 2:
                            act.wait_ge(s_yps, 2 * (t - 1))
                        act.copy(o_hi[:, t % 2, :], ps_o[:, :]).then_inc(s_ohi, 1)

                    for t in range(TILES + 2):
                        if t < TILES:
                            split_x(t)
                        if 1 <= t <= TILES:
                            theta_hi(t - 1)
                        if t >= 2:
                            stack_phi(t - 2)
                            split_g(t - 2)
                    for c in range(NC + 2):
                        exp_sum(c)
                    copy_row(0)
                    exponentiate(0)
                    for t in range(TILES):
                        for b in range(MB):
                            q = t * MB + b
                            c = NC * (t + 1) + 2 + (b - 1) // 2
                            if q + 1 < LAST:
                                exponentiate(q + 1)
                            if b == 0 and t >= 1:
                                split_o(t - 1)
                            split_e(q)
                            if b % 2 == 1 and c < CHUNKS:
                                exp_sum(c)
                            if b == 5 and t + 1 < TILES:
                                copy_row(t + 1)
                    split_o(TILES - 1)

                @block.vector
                def _(dve):
                    def split_x(t):
                        dve.wait_ge(s_xhi, t + 1)
                        dve.tensor_tensor(x_lo[:, t % 2, 0, :], x_raw[:, t % 2, 0, :],
                                          x_hi[:, t % 2, 0, :].bitcast(F32), ALU.subtract).then_inc(s_xlo_v, 1)

                    def window(ap):
                        return ap.rearrange("p (r h w v) -> p r w h v", r=ROWS // 2, h=2, v=2)

                    def pooled(ap):
                        return ap.rearrange("p (r w) -> p r w", r=ROWS // 2)

                    def pool_phi(t):
                        dve.wait_ge(s_tp, t + 1)
                        if t >= 2:
                            dve.wait_ge(s_phihi, t - 1)
                            dve.wait_ge(s_philo, t - 1)
                        dve.tensor_reduce(pooled(phi_pool[SHIFT:, t % 2, :]),
                                          window(ps_scores[SHIFT:, (t % 2) * NT:(t % 2 + 1) * NT]),
                                          AX.XY, ALU.max).then_inc(s_phipool, 1)

                    def pool_g(t):
                        dve.wait_ge(s_g, t + 1)
                        if t >= 2:
                            dve.wait_ge(s_gT, t - 1)
                        dve.tensor_reduce(pooled(g_pool[:, t % 2, :]), window(ps_st[:, t % 2, :]),
                                          AX.XY, ALU.max).then_inc(s_gpool, 1)

                    def theta_lo(t):
                        dve.wait_ge(s_th_hi, t + 1)
                        dst = theta[DA:2 * DA, t * NT:(t + 1) * NT]
                        dve.tensor_tensor(dst, ps_scores[DA:2 * DA, (t % 2) * NT:(t % 2 + 1) * NT],
                                          dst.bitcast(F32), ALU.subtract).then_inc(s_th_lo, 1)

                    def split_g(t):
                        bank = ps_o[:, 0:P] if t % 2 == 0 else ps_y[:, 0, 0:P]
                        dve.wait_ge(s_ghi, t + 1)
                        dve.tensor_tensor(g_lo[:, t, :], bank, g_hi[:, t, :].bitcast(F32),
                                          ALU.subtract).then_inc(s_glo, 1)

                    def phi_lo(t):
                        dve.wait_ge(s_phihi, t + 1)
                        dve.tensor_tensor(phi[2 * DA:3 * DA, t * P:(t + 1) * P], phi_pool[SHIFT:, t % 2, :],
                                          phi_hi[SHIFT:, t % 2, :].bitcast(F32), ALU.subtract).then_inc(s_philo, 1)

                    def maximum(c):
                        t, j = divmod(c, NC)
                        dve.wait_ge(s_scores, c + 1)
                        dve.tensor_reduce(neg_max[:, t % RING, j:j + 1], ps_scores[:, :], AX.X, ALU.max,
                                          negate=True).then_inc(s_max, 1)

                    def split_e(q):
                        dve.wait_ge(s_ehi, q + 1)
                        if q >= RING:
                            dve.wait_ge(s_av, q - RING + 1)
                        dve.tensor_tensor(e_lo[:, q % RING, :], e_val[:, q % RING, :],
                                          e_hi[:, q % RING, :].bitcast(F32), ALU.subtract).then_inc(s_elo_v, 1)

                    def split_o(t):
                        dve.wait_ge(s_ohi, t + 1)
                        dve.tensor_tensor(o_lo[:, t % 2, :], ps_o[:, :], o_hi[:, t % 2, :].bitcast(F32),
                                          ALU.subtract).then_inc(s_olo, 1)

                    def weight_scale(t):
                        dve.wait_ge(s_z, NC * (t + 1))
                        dve.reciprocal(recip[:, t % 2, :], total[:, t % RING, :]).then_inc(s_recip, 1)
                        dve.wait_ge(s_recip, t + 1)
                        dve.tensor_scalar(scale[:, t % 2, :], recip[:, t % 2, :], sig[:, 0:1], None,
                                          ALU.mult).then_inc(s_scale, 1)

                    def residual(t, half):
                        if half == 0:
                            dve.wait_ge(s_scale, t + 1)
                            dve.wait_ge(s_xn[t % 3], 16 * (t // 3 + 1))
                            if t >= 3:
                                dve.wait_ge(s_yst[t % 3], 16 * (t // 3))
                                dve.wait_ge(s_ylo, t - 2)
                                dve.wait_ge(s_ysum, t - 2)
                        dve.wait_ge(s_yps, 2 * t + half + 1)
                        for k in range(2):
                            j = 2 * half + k
                            last = dve.scalar_tensor_tensor(y_val[:, t % 3, j, :], ps_y[:, k, :],
                                                            scale[:, t % 2, j:j + 1], x_nat[:, t % 3, j, :],
                                                            ALU.mult, ALU.add)
                        last.then_inc(s_y, 1)

                    def split_y(t):
                        dve.wait_ge(s_y, 2 * (t + 1))
                        if t >= 2:
                            dve.wait_ge(s_cov, t - 1)
                        dve.tensor_copy(y_split[:, t % 2, :, 0:C], y_val[:, t % 3, :, :]).then_inc(s_yhi, 1)

                    for t in range(TILES + 2):
                        if t < TILES:
                            split_x(t)
                        if 1 <= t <= TILES:
                            pool_phi(t - 1)
                            theta_lo(t - 1)
                            pool_g(t - 1)
                        if t >= 2:
                            phi_lo(t - 2)
                            split_g(t - 2)
                    for c in range(NC + 2):
                        maximum(c)
                    for t in range(TILES):
                        for b in range(MB):
                            q = t * MB + b
                            c = NC * (t + 1) + 2 + b // 2
                            if b == 0 and t >= 1:
                                split_o(t - 1)
                            if not pool_takes(q):
                                split_e(q)
                            if b % 2 == 0 and c < CHUNKS:
                                maximum(c)
                            if b == 1:
                                weight_scale(t)
                            if b in (1, 3) and t >= 1:
                                residual(t - 1, b // 2)
                            if b == 4 and t >= 1:
                                split_y(t - 1)
                    split_o(TILES - 1)
                    residual(TILES - 1, 0)
                    residual(TILES - 1, 1)
                    split_y(TILES - 1)

                @block.gpsimd
                def _(pool):
                    def split_x(t):
                        pool.wait_ge(s_xhi, t + 1)
                        pool.tensor_tensor(x_lo[:, t % 2, 1, :], x_raw[:, t % 2, 1, :],
                                           x_hi[:, t % 2, 1, :].bitcast(F32), ALU.subtract).then_inc(s_xlo_p, 1)

                    def split_e(q):
                        pool.wait_ge(s_ehi, q + 1)
                        if q >= RING:
                            pool.wait_ge(s_av, q - RING + 1)
                        pool.tensor_tensor(e_lo[:, q % RING, :], e_val[:, q % RING, :],
                                           e_hi[:, q % RING, :].bitcast(F32), ALU.subtract).then_inc(s_elo_p, 1)

                    def sum_y(t):
                        pool.wait_ge(s_y, 2 * (t + 1))
                        if t >= 1:
                            pool.wait_ge(s_ysum, t)
                        pool.tensor_tensor(y_sum[:, :, :], y_sum[:, :, :], y_val[:, t % 3, :, :],
                                           ALU.add).then_inc(s_ysum, 1)

                    def split_y(t):
                        pool.wait_ge(s_yhi, t + 1)
                        pool.tensor_tensor(y_split[:, t % 2, :, C:], y_val[:, t % 3, :, :],
                                           y_split[:, t % 2, :, 0:C].bitcast(F32), ALU.subtract
                                           ).then_inc(s_ylo, 1)

                    for t in range(TILES):
                        split_x(t)
                    for t in range(TILES):
                        for b in range(MB):
                            q = t * MB + b
                            if pool_takes(q):
                                split_e(q)
                            if b == 4 and t >= 1:
                                split_y(t - 1)
                            if b == 5 and t >= 1:
                                sum_y(t - 1)
                    split_y(TILES - 1)
                    sum_y(TILES - 1)

            nc.all_engine_barrier(sems_to_clear=range(cleared[0].num, cleared[-1].num + 1))

        s_f = sem("s_f")
        row_s = sb("row_s", [1, C])
        mean = sb("mean", [P, CC])
        hl = sb("hl", [P, 3, P])
        a_mat = sb("a_mat", [P, 3, P])
        elim = sb("elim", [P, 2 * P])
        rinv = sb("rinv", [P, 1])
        mult = sb("mult", [P, 1])
        diag = sb("diag", [P, P])
        dcol = sb("dcol", [P, 2])
        w_inv = sb("w_inv", [P, 2, P])
        w_invT = sb("w_invT", [P, 2, P])
        b_mat = sb("b_mat", [P, P])
        x_mat = sb("x_mat", [P, P])
        w_10 = sb("w_10", [P, P])
        wg = sb("wg", [P, 3, P])
        wgT_hi = sb("wgT_hi", [P, 3, P], F32R)
        wgT_lo = sb("wgT_lo", [P, 3, P], F32R)
        wgT = sb("wgT", [P, 3, P])
        bias = sb("bias", [P, CC])

        with nc.Block() as block:
            plan = whitening_plan()

            @block.tensor
            def _(pe):
                def after(n):
                    pe.wait_ge(s_f, n)

                pe.matmul(ps_o[0:1, 0:C], ones[:, 0:1], y_sum[:, 0, :], start=True, stop=False)
                for j in range(1, NC):
                    last = pe.matmul(ps_o[0:1, 0:C], ones[:, 0:1], y_sum[:, j, :], start=False, stop=(j == NC - 1))
                last.then_inc(s_f, 1)
                for a in range(CC):
                    for j in range(NC):
                        last = pe.matmul(ps_y[:, 0, a:a + 1], y_sum[:, j, a * P:(a + 1) * P], ones[:, 0:1],
                                         start=(j == 0), stop=(j == NC - 1))
                last.then_inc(s_f, 1)
                after(plan["rows"])
                for a in range(CC):
                    last = pe.matmul(ps_st[:, a, 0:C], row_s[0:1, a * P:(a + 1) * P], row_s[0:1, :],
                                     start=True, stop=True)
                last.then_inc(s_f, 1)
                after(plan["hl"])
                for k in range(3):
                    last = pe.transpose(ps_scores[:, k * P:(k + 1) * P], hl[:, k, :], ident[:, :])
                last.then_inc(s_f, 1)
                for half in range(2):
                    base = plan["elim"][half]
                    for k in range(P):
                        after(base + 1 + 4 * k)
                        pe.matmul(ps_st[:, k % 2, 0:P + 1], ident[:, k:k + 1].to_broadcast([P, P]),
                                  elim[:, k:k + P + 1], start=True, stop=True).then_inc(s_f, 1)
                    if half == 0:
                        after(plan["w0"])
                        pe.transpose(ps_o[:, 0:P], w_inv[:, 0, :], ident[:, :]).then_inc(s_f, 1)
                        after(plan["w0"] + 2)
                        pe.matmul(ps_o[:, P:2 * P], w_invT[:, 0, :], a_mat[:, 1, :], start=True,
                                  stop=True).then_inc(s_f, 1)
                        after(plan["w0"] + 4)
                        pe.matmul(ps_y[:, 0, 0:P], b_mat[:, :], b_mat[:, :], start=True, stop=True)
                        pe.matmul(ps_y[:, 1, 0:P], b_mat[:, :], w_inv[:, 0, :], start=True,
                                  stop=True).then_inc(s_f, 1)
                    else:
                        after(plan["w1"])
                        pe.transpose(ps_o[:, 0:P], w_inv[:, 1, :], ident[:, :]).then_inc(s_f, 1)
                        after(plan["w1"] + 2)
                        pe.matmul(ps_o[:, P:2 * P], w_invT[:, 1, :], x_mat[:, :], start=True,
                                  stop=True).then_inc(s_f, 1)
                after(plan["wg"])
                for k in range(3):
                    last = pe.transpose(ps_st[:, 0, k * P:(k + 1) * P], wg[:, k, :], ident[:, :])
                last.then_inc(s_f, 1)
                after(plan["wgT"])
                pe.matmul(ps_y[:, 0, 0:1], wgT[:, 0, :], mean[:, 0:1], start=True, stop=True)
                pe.matmul(ps_y[:, 0, 1:2], wgT[:, 1, :], mean[:, 0:1], start=True, stop=False)
                pe.matmul(ps_y[:, 0, 1:2], wgT[:, 2, :], mean[:, 1:2], start=False, stop=True).then_inc(s_f, 1)

            @block.vector
            def _(dve):
                n = [2]

                def step(ins):
                    ins.then_inc(s_f, 1)
                    n[0] += 1

                def now():
                    dve.wait_ge(s_f, n[0])

                def other():
                    n[0] += 1
                    now()

                now()
                step(dve.tensor_copy(row_s[0:1, :], ps_o[0:1, 0:C]))
                step(dve.tensor_scalar(mean[:, :], ps_y[:, 0, 0:CC], 1.0 / TOTAL, None, ALU.mult))
                assert n[0] == plan["rows"]
                other()
                for k, (a, col) in enumerate(((0, 2 * P), (1, P), (1, 2 * P))):
                    step(dve.tensor_copy(hl[:, k, :], ps_cov[:, a, col:col + P]))
                assert n[0] == plan["hl"]
                other()
                srcs = ((ps_cov[:, 0, 0:P], hl[:, 0, :]), (ps_cov[:, 0, P:2 * P], ps_cov[:, 0, 3 * P:4 * P]),
                        (ps_cov[:, 1, 0:P], hl[:, 2, :]))
                for k, (hh, own) in enumerate(srcs):
                    outer = ps_st[:, 0, 0:P] if k == 0 else (ps_st[:, 0, P:2 * P] if k == 1 else ps_st[:, 1, P:2 * P])
                    dst = a_mat[:, k, :]
                    step(dve.tensor_copy(dst, hh))
                    now()
                    step(dve.tensor_tensor(dst, own, dst, ALU.add))
                    now()
                    step(dve.tensor_tensor(dst, ps_scores[:, k * P:(k + 1) * P], dst, ALU.add))
                    now()
                    step(dve.scalar_tensor_tensor(dst, outer, -1.0 / TOTAL, dst, ALU.mult, ALU.add))
                    now()
                    step(dve.tensor_scalar(dst, dst, (1.0 - WHITEN_EPS) / (TOTAL - 1.0), None, ALU.mult))
                    now()
                    if k != 1:
                        step(dve.scalar_tensor_tensor(dst, ident[:, :], WHITEN_EPS, dst, ALU.mult, ALU.add))
                        now()
                for half in range(2):
                    src = a_mat[:, 0, :] if half == 0 else a_mat[:, 2, :]
                    assert n[0] == plan["elim"][half] - 1, (n[0], plan["elim"])
                    step(dve.tensor_copy(elim[:, 0:P], src))
                    step(dve.tensor_copy(elim[:, P:], ident[:, :]))
                    for k in range(P):
                        other()
                        row = ps_st[:, k % 2, 0:P + 1]
                        step(dve.reciprocal(rinv[:, :], row[:, 0:1]))
                        now()
                        step(dve.scalar_tensor_tensor(mult[:, :], elim[:, k:k + 1], below[:, k:k + 1], rinv[:, :],
                                                      ALU.mult, ALU.mult))
                        now()
                        cols = elim[:, k:k + P + 1]
                        step(dve.scalar_tensor_tensor(cols, row, mult[:, 0:1], cols, ALU.mult, ALU.add))
                    now()
                    step(dve.tensor_tensor(diag[:, :], elim[:, 0:P], ident[:, :], ALU.mult))
                    now()
                    step(dve.tensor_reduce(dcol[:, 0:1], diag[:, :], AX.X, ALU.add))
                    now()
                    step(dve.reciprocal(dcol[:, 1:2], dcol[:, 0:1]))
                    other()
                    step(dve.tensor_scalar(w_inv[:, half, :], elim[:, P:], mult[:, 0:1], None, ALU.mult))
                    assert n[0] == plan["w0" if half == 0 else "w1"], (n[0], plan)
                    other()
                    step(dve.tensor_copy(w_invT[:, half, :], ps_o[:, 0:P]))
                    other()
                    if half == 0:
                        step(dve.tensor_copy(b_mat[:, :], ps_o[:, P:2 * P]))
                        other()
                        step(dve.tensor_copy(x_mat[:, :], ps_y[:, 1, 0:P]))
                        step(dve.scalar_tensor_tensor(a_mat[:, 2, :], ps_y[:, 0, 0:P], -1.0, a_mat[:, 2, :],
                                                      ALU.mult, ALU.add))
                        now()
                    else:
                        step(dve.tensor_scalar(w_10[:, :], ps_o[:, P:2 * P], -1.0, None, ALU.mult))
                        now()
                step(dve.tensor_scalar(wg[:, 0, :], w_inv[:, 0, :], gam[:, 0:1], None, ALU.mult))
                step(dve.tensor_scalar(wg[:, 1, :], w_10[:, :], gam[:, 1:2], None, ALU.mult))
                step(dve.tensor_scalar(wg[:, 2, :], w_inv[:, 1, :], gam[:, 1:2], None, ALU.mult))
                assert n[0] == plan["wg"], (n[0], plan)
                other()
                step(dve.tensor_copy(wgT[:, :, :], ps_st[:, 0, 0:3 * P].rearrange("p (k c) -> p k c", k=3)))
                now()
                step(dve.tensor_copy(wgT_hi[:, :, :], wgT[:, :, :]))
                now()
                step(dve.tensor_tensor(wgT_lo[:, :, :], wgT[:, :, :], wgT_hi[:, :, :].bitcast(F32), ALU.subtract))
                assert n[0] == plan["wgT"], (n[0], plan)
                other()
                step(dve.scalar_tensor_tensor(bias[:, :], ps_y[:, 0, 0:CC], -1.0, bet[:, :], ALU.mult, ALU.add))

            @block.scalar
            def _(act):
                for half in range(2):
                    act.wait_ge(s_f, plan["w0" if half == 0 else "w1"] - 2)
                    act.activation(mult[:, :], dcol[:, 1:2], ACT.Sqrt).then_inc(s_f, 1)

        whiten(nc, ctx, yN, outT, x_nat, ps_scores, ps_st, ps_o, ps_y, ps_cov, ident, wgT_hi, wgT_lo, bias,
               x_hi, x_lo, B * TILES, TILES)


def whitening_plan():
    plan = {"rows": 4}
    plan["hl"] = plan["rows"] + 1 + 3
    at = plan["hl"] + 1 + 3 * 5 + 2
    plan["elim"] = [at + 1]
    at += 2 + 4 * P
    plan["w0"] = at + 5
    at = plan["w0"] + 7
    plan["elim"].append(at + 1)
    at += 2 + 4 * P
    plan["w1"] = at + 5
    plan["wg"] = plan["w1"] + 4 + 3
    plan["wgT"] = plan["wg"] + 1 + 3
    return plan


def whiten(nc, ctx, yN, outT, y_in, ps_scores, ps_st, ps_o, ps_y, ps_cov, ident, w_hi, w_lo, bias,
           yT_hi, yT_lo, tiles, per_image):
    C = yN.shape[3]
    CC = C // P

    def sem(name):
        return ctx.enter_context(nc.semaphore(name))

    out_sb = ctx.enter_context(nc.sbuf_tensor("out_sb", [P, 2, CC, NT], F32))
    s_in = [sem("w_in0"), sem("w_in1")]
    s_turn = sem("w_turn")
    s_hi, s_lo = sem("w_hi"), sem("w_lo")
    s_mm = sem("w_mm")
    s_outa, s_outv = sem("w_outa"), sem("w_outv")
    s_st = [sem("w_st0"), sem("w_st1")]
    turned = (ps_scores[:, :].rearrange("p (a n) -> p a n", a=CC), ps_st[:, :, :])
    prod = ((ps_o[:, :], ps_y[:, :, :].rearrange("p a c -> p (a c)")), (ps_cov[:, 0, :], ps_cov[:, 1, :]))

    with nc.Block() as block:
        @block.sync
        def _(sp):
            pairs = yN.rearrange("(u s) j p c -> u s p j c", s=2)

            def load(pair, slot):
                sp.dma_start(y_in[:, slot, :, :], pairs[pair, slot]).then_inc(s_in[slot], 16)

            load(0, 0)
            load(0, 1)
            with sp.Fori(1, tiles // 2) as u:
                for slot in range(2):
                    sp.wait_ge(s_turn, 2 * u - 1 + slot)
                    load(u, slot)

        @block.gpsimd
        def _(pool):
            with pool.Fori(0, tiles // per_image) as img:
                for k in range(per_image):
                    pool.wait_ge(s_outa, img * per_image + k + 1)
                    pool.wait_ge(s_outv, img * per_image + k + 1)
                    pool.dma_start(outT[img, :, k * NT:(k + 1) * NT].rearrange("(a p) n -> p a n", p=P),
                                   out_sb[:, k % 2, :, :]).then_inc(s_st[k % 2], 16)
            for slot in range(2):
                pool.wait_ge(s_st[slot], 16 * (tiles // 2))

        @block.tensor
        def _(pe):
            def turn(slot, landed, free):
                pe.wait_ge(s_in[slot], landed)
                if free is not None:
                    pe.wait_ge(s_lo, free)
                for a in range(CC):
                    for j in range(NC):
                        last = pe.transpose(turned[slot][:, a, j * P:(j + 1) * P],
                                            y_in[:, slot, j, a * P:(a + 1) * P], ident[:, :])
                last.then_inc(s_turn, 1)

            def product(slot, split, free):
                if free is not None:
                    pe.wait_ge(s_outa, free)
                    pe.wait_ge(s_outv, free)
                pe.wait_ge(s_lo, split)
                blocks = (((0, 0),), ((1, 0), (2, 1)))
                for a in range(CC):
                    dst = prod[slot][a]
                    for k, (w, h) in enumerate(blocks[a]):
                        hi, lo = yT_hi[:, slot, h, :], yT_lo[:, slot, h, :]
                        pe.matmul(dst, w_hi[:, w, :], hi, start=(k == 0), stop=False)
                        pe.matmul(dst, w_hi[:, w, :], lo, start=False, stop=False)
                        last = pe.matmul(dst, w_lo[:, w, :], hi, start=False, stop=(k == len(blocks[a]) - 1))
                last.then_inc(s_mm, 1)

            turn(0, 16, None)
            turn(1, 16, None)
            product(0, 1, None)
            turn(0, 32, 1)
            product(1, 2, None)
            turn(1, 32, 2)
            product(0, 3, 1)
            with pe.Fori(4, tiles, 2) as i:
                turn(0, i * 8 + 16, i - 1)
                product(1, i, i - 2)
                turn(1, i * 8 + 16, i)
                product(0, i + 1, i - 1)
            product(1, tiles, tiles - 2)

        @block.scalar
        def _(act):
            def split(slot, turns, used):
                act.wait_ge(s_turn, turns)
                if used is not None:
                    act.wait_ge(s_mm, used)
                act.copy(yT_hi[:, slot, :, :], turned[slot]).then_inc(s_hi, 1)

            def finish(slot, products, stored):
                act.wait_ge(s_mm, products)
                if stored is not None:
                    act.wait_ge(s_st[slot], stored)
                act.activation(out_sb[:, slot, 0, :], prod[slot][0], ACT.Identity,
                               bias=bias[:, 0:1]).then_inc(s_outa, 1)

            split(0, 1, None)
            split(1, 2, None)
            finish(0, 1, None)
            split(0, 3, 1)
            finish(1, 2, None)
            split(1, 4, 2)
            finish(0, 3, 16)
            with act.Fori(4, tiles, 2) as i:
                split(0, i + 1, i - 1)
                finish(1, i, i * 8 - 16)
                split(1, i + 2, i)
                finish(0, i + 1, i * 8)
            finish(1, tiles, 8 * tiles - 16)

        @block.vector
        def _(dve):
            def split(slot, his, used):
                dve.wait_ge(s_hi, his)
                if used is not None:
                    dve.wait_ge(s_mm, used)
                dve.tensor_tensor(yT_lo[:, slot, :, :], turned[slot], yT_hi[:, slot, :, :].bitcast(F32),
                                  ALU.subtract).then_inc(s_lo, 1)

            def finish(slot, products, stored):
                dve.wait_ge(s_mm, products)
                if stored is not None:
                    dve.wait_ge(s_st[slot], stored)
                dve.tensor_scalar(out_sb[:, slot, 1, :], prod[slot][1], bias[:, 1:2], None,
                                  ALU.add).then_inc(s_outv, 1)

            split(0, 1, None)
            split(1, 2, None)
            finish(0, 1, None)
            split(0, 3, 1)
            finish(1, 2, None)
            split(1, 4, 2)
            finish(0, 3, 16)
            with dve.Fori(4, tiles, 2) as i:
                split(0, i + 1, i - 1)
                finish(1, i, i * 8 - 16)
                split(1, i + 2, i)
                finish(0, i + 1, i * 8)
            finish(1, tiles, 8 * tiles - 16)


def kernel(**inputs):
    import numpy as np
    import concourse.bacc as bacc
    from concourse.bass_utils import run_bass_kernel_spmd

    x = np.asarray(inputs["x"])
    B, H, W, C = x.shape
    N = H * W
    flat = x.reshape(B, N, C)
    arrays = {
        "xT": np.ascontiguousarray(flat.transpose(0, 2, 1)),
        "xN": np.ascontiguousarray(flat).reshape(B * N // NT, NT // P, P, C),
        "w_theta": np.asarray(inputs["L0_conv_w_theta"]),
        "w_phi": np.asarray(inputs["L0_conv_w_phi"]),
        "w_g": np.asarray(inputs["L0_conv_w_g"]),
        "w_out": np.asarray(inputs["L0_conv_w_out"]),
        "sigma": np.asarray(inputs["L0_conv_sigma"]).reshape(1),
        "gamma": np.asarray(inputs["L1_conv_gamma"]),
        "beta": np.asarray(inputs["L1_conv_beta"]),
    }
    nc = bacc.Bacc("TRN2", target_bir_lowering=False, num_devices=1)
    args = [nc.dram_tensor(f"in_{k}", a.shape, mybir.dt.from_np(a.dtype), kind="ExternalInput").ap()
            for k, a in arrays.items()]
    outT = nc.dram_tensor("out", [B, C, N], F32, kind="ExternalOutput").ap()
    attention_whitening_kernel(nc, *args, outT)
    r = run_bass_kernel_spmd(nc, [{f"in_{k}": a for k, a in arrays.items()}], core_ids=[0])
    got = r.results[0]["out"]
    return np.ascontiguousarray(got.reshape(B, C, N).transpose(0, 2, 1)).reshape(B, H, W, C)
```

```python
from contextlib import ExitStack

import concourse.bass as bass
from concourse import mybir

F32 = mybir.dt.float32
F32R = mybir.dt.float32r
ALU = mybir.AluOpType
ACT = mybir.ActivationFunctionType
AX = mybir.AxisListType

P = 128
NT = 512
NC = NT // P
WHITEN_EPS = 1e-3
NEWTON_STEPS = 4
SETTLED = 1e-9


def attention_whitening_kernel(nc, xT, xN, w_theta, w_phi, w_g, w_out, sigma, gamma, beta, outT):
    B, TILES, _P, CC, _NT = xT.shape
    C, N = CC * P, TILES * NT
    DA = w_theta.shape[1]
    DG = w_g.shape[1]
    WIDTH = 64
    ROWS = NT // WIDTH
    M = N // 4
    MB = M // P
    assert MB == TILES and DG == P and 3 * DA + DA == P
    TOTAL = B * N
    SHIFT = 3 * DA
    STEPS = TILES * MB
    PAIR = 2
    CHUNKS = TILES * NC
    RING = 6
    SPLIT_RING = 3
    AHEAD = 4
    SPLIT_AHEAD = 3
    LEAD = 10
    CHUNK_STEPS = range(0, STEPS, STEPS // CHUNKS)
    PROJ_STEPS = (1, 7, 11, 17, 21, 27, 31, 37)
    MOMENT_STEPS = (13, 29, 45, 59)
    TURN_STEP = 49
    Y_RING = 4
    TURNS = 4
    UPPER = 2 * C - P
    SETUP_LOADS = 5 + 2 * CC

    yN = nc.dram_tensor("y_spill", [B * TILES, P, NC, C], F32, kind="Internal").ap()

    with ExitStack() as ctx:
        def sb(name, shape, dt=F32):
            return ctx.enter_context(nc.sbuf_tensor(name, shape, dt))

        def ps(name, shape):
            return ctx.enter_context(nc.psum_tensor(name, shape, F32))

        def sem(name):
            return ctx.enter_context(nc.semaphore(name))

        ps_scores = ps("ps_scores", [P, 2, M])
        ps_st = ps("ps_st", [P, 2, NT])
        ps_oy = ps("ps_oy", [P, 2, NT])

        w_t = sb("w_t", [P, CC, DA])
        w_p = sb("w_p", [P, CC, DA])
        w_tp_hi = sb("w_tp_hi", [P, CC, P], F32R)
        w_tp_lo = sb("w_tp_lo", [P, CC, P], F32R)
        w_gs = sb("w_gs", [P, CC, DG])
        w_g_hi = sb("w_g_hi", [P, CC, DG], F32R)
        w_g_lo = sb("w_g_lo", [P, CC, DG], F32R)
        w_o = sb("w_o", [P, C])
        w_o_hi = sb("w_o_hi", [P, C], F32R)
        w_o_lo = sb("w_o_lo", [P, C], F32R)
        sig = sb("sig", [P, 1])
        gam = sb("gam", [P, CC])
        bet = sb("bet", [P, CC])
        ident = sb("ident", [P, P])
        ident_r = sb("ident_r", [P, P], F32R)
        ones = sb("ones", [P, P])
        below = sb("below", [P, P])
        moment = sb("moment", [P, 2, NT])

        x_raw = sb("x_raw", [P, 2, CC, NT])
        x_hi = sb("x_hi", [P, 2, CC, NT], F32R)
        x_lo = sb("x_lo", [P, 2, CC, NT], F32R)
        theta = sb("theta", [P, 2, N], F32R)
        phi = sb("phi", [P, 2, M], F32R)
        phi_pool = sb("phi_pool", [P, 2, P])
        phi_hi = sb("phi_hi", [P, 2, P], F32R)
        g_pool = sb("g_pool", [P, MB, P])
        g_val = sb("g_val", [P, 2, MB, DG])
        g_hi = sb("g_hi", [P, 2, MB, DG], F32R)
        g_lo = sb("g_lo", [P, 2, MB, DG], F32R)
        neg_max = sb("neg_max", [P, TURNS, NC], F32R)
        total = sb("total", [P, TURNS, NC])
        scale = sb("scale", [P, 2, NC])
        recip = sb("recip", [P, 2, NC])
        dump = sb("dump", [P, 2, M], mybir.dt.bfloat16)
        e_val = sb("e_val", [P, RING, NT])
        e_hi = sb("e_hi", [P, SPLIT_RING, NT], F32R)
        e_lo = sb("e_lo", [P, SPLIT_RING, NT], F32R)
        o_hi = sb("o_hi", [P, 2, NT], F32R)
        o_lo = sb("o_lo", [P, 2, NT], F32R)
        x_nat = sb("x_nat", [P, 3, NC, C])
        y_val = sb("y_val", [P, 3, NC, C])
        y_split = sb("y_split", [P, Y_RING, NC, 2 * C], F32R)
        y_sum = sb("y_sum", [P, NC, C])

        moments_flat = moment[:, :, :].rearrange("p a n -> p (a n)")[:, 0:NT + UPPER]

        s_setup_dma = sem("s_setup_dma")
        s_const0 = sem("s_const0")
        s_const = sem("s_const")
        s_whi = sem("s_whi")
        s_wlo = sem("s_wlo")
        s_first = sem("s_first")
        s_first_hi = sem("s_first_hi")
        s_first_lo = sem("s_first_lo")
        cleared = []

        def isem(name):
            s = sem(name)
            cleared.append(s)
            return s

        s_xt = [isem("s_xt0"), isem("s_xt1")]
        s_xhi = isem("s_xhi")
        s_xlo_p = isem("s_xlo_p")
        s_tp = isem("s_tp")
        s_g = isem("s_g")
        s_th_hi = isem("s_th_hi")
        s_th_lo = isem("s_th_lo")
        s_phipool = isem("s_phipool")
        s_gpool = isem("s_gpool")
        s_gT = isem("s_gT")
        s_ghi = isem("s_ghi")
        s_glo = isem("s_glo")
        s_phihi = isem("s_phihi")
        s_phi = isem("s_phi")
        s_philo = isem("s_philo")
        s_scores = isem("s_scores")
        s_max = isem("s_max")
        s_z = isem("s_z")
        s_rowT = isem("s_rowT")
        s_row = isem("s_row")
        s_st = isem("s_st")
        s_e = isem("s_e")
        s_ehi = isem("s_ehi")
        s_elo_v = isem("s_elo_v")
        s_elo_p = isem("s_elo_p")
        s_av = isem("s_av")
        s_ohi = isem("s_ohi")
        s_olo = isem("s_olo")
        s_yps = isem("s_yps")
        s_recip = isem("s_recip")
        s_scale = isem("s_scale")
        s_y = isem("s_y")
        s_yhi = isem("s_yhi")
        s_ylo = isem("s_ylo")
        s_ysum = isem("s_ysum")
        s_mom = isem("s_mom")
        s_momadd = isem("s_momadd")
        s_gval = isem("s_gval")
        s_xn = [isem(f"s_xn{k}") for k in range(3)]
        s_yst = [isem(f"s_yst{k}") for k in range(3)]

        with nc.Block() as block:
            @block.sync
            def _(sp):
                for dst, src in ((w_t, w_theta), (w_p, w_phi), (w_gs, w_g)):
                    sp.dma_start(dst[:, :, :], src.rearrange("(a p) d -> p a d", p=P)).then_inc(s_setup_dma, 16)
                for t in range(2):
                    sp.dma_start(x_raw[:, t, :, :], xT[0, t]).then_inc(s_first, 16)
                sp.dma_start(w_o[:, :], w_out).then_inc(s_setup_dma, 16)
                sp.dma_start(sig[:, :], sigma.partition_broadcast(P)).then_inc(s_setup_dma, 16)
                for dst, src in ((gam, gamma), (bet, beta)):
                    for a in range(CC):
                        sp.dma_start(dst[:, a:a + 1],
                                     src[a * P:(a + 1) * P].rearrange("(p o) -> p o", o=1)).then_inc(s_setup_dma, 16)
                sp.wait_ge(s_setup_dma, 16 * SETUP_LOADS)

            @block.gpsimd
            def _(pool):
                pool.memset(ident[:, :], 0.0).then_inc(s_const0, 1)
                pool.memset(below[:, :], 0.0).then_inc(s_const0, 1)
                pool.memset(ones[:, :], 1.0).then_inc(s_const, 1)
                pool.memset(y_sum[:, :, :], 0.0).then_inc(s_const, 1)
                pool.memset(moment[:, :, :], 0.0).then_inc(s_const, 1)
                pool.wait_ge(s_const0, 2)
                pool.affine_select(out=ident[:, :], in_=ident[:, :], compare_op=ALU.not_equal, fill=1.0,
                                   base=0, pattern=[[-1, P]], channel_multiplier=1).then_inc(s_const, 1)
                pool.affine_select(out=below[:, :], in_=below[:, :], compare_op=ALU.is_ge, fill=-1.0,
                                   base=0, pattern=[[1, P]], channel_multiplier=-1).then_inc(s_const, 1)

            @block.vector
            def _(dve):
                dve.memset(y_split[:, Y_RING - 2:, :, :].bitcast(F32), 0.0).then_inc(s_const, 1)
                dve.wait_ge(s_const, 6)
                dve.tensor_copy(ident_r[:, :], ident[:, :]).then_inc(s_const, 1)
                for buf in range(2):
                    dve.tensor_copy(phi[SHIFT:SHIFT + 1, buf, :],
                                    ones[SHIFT:SHIFT + 1, 0:1].to_broadcast([1, M])).then_inc(s_const, 1)
                dve.wait_ge(s_setup_dma, 16 * SETUP_LOADS)
                tp = [(w_t[:, :, :], slice(k * DA, (k + 1) * DA)) for k in range(3)] + [(w_p[:, :, :], slice(3 * DA, P))]
                pairs = [(raw, w_tp_hi[:, :, cols], w_tp_lo[:, :, cols]) for raw, cols in tp]
                pairs += [(w_gs[:, :, :], w_g_hi[:, :, :], w_g_lo[:, :, :]), (w_o[:, :], w_o_hi[:, :], w_o_lo[:, :])]
                for raw, hi, _lo in pairs:
                    dve.tensor_copy(hi, raw).then_inc(s_whi, 1)
                for k, (raw, hi, lo) in enumerate(pairs):
                    dve.wait_ge(s_whi, k + 1)
                    dve.tensor_tensor(lo, raw, hi.bitcast(F32), ALU.subtract).then_inc(s_wlo, 1)

                for t in range(2):
                    dve.wait_ge(s_first_hi, t + 1)
                    dve.tensor_tensor(x_lo[:, t, :, :], x_raw[:, t, :, :], x_hi[:, t, :, :].bitcast(F32),
                                      ALU.subtract).then_inc(s_first_lo, 1)

            @block.scalar
            def _(act):
                act.wait_ge(s_first, 32)
                for t in range(2):
                    act.copy(x_hi[:, t, :, :], x_raw[:, t, :, :]).then_inc(s_first_hi, 1)

        def is_split(q):
            return q % 2 == 1

        def pool_takes(q):
            return q % 4 == 3

        def splits(q):
            return sum(is_split(k) for k in range(q))

        def split_before(q, n):
            earlier = [k for k in range(q) if is_split(k)]
            return earlier[-n] if len(earlier) >= n else None

        def dve_los(q):
            return sum(is_split(k) and not pool_takes(k) for k in range(q))

        def pool_los(q):
            return sum(pool_takes(k) for k in range(q))

        def moments_of(pe, acc, slot, first):
            for j in range(NC):
                y2 = y_split[:, slot, j, :]
                flags = dict(start=(first and j == 0), stop=(not first and j == NC - 1))
                pe.matmul(acc[:, 0:NT], y2[:, 0:P], y2, **flags)
                last = pe.matmul(acc[:, NT:NT + UPPER], y2[:, P:2 * P], y2[:, P:], **flags)
            return last

        def image_items():
            items = [(s, "chunk") for s in CHUNK_STEPS] + [(s, "project") for s in PROJ_STEPS]
            items += [(s, "moments") for s in MOMENT_STEPS] + [(TURN_STEP, "turn_g")]
            assert len(dict(items)) == len(items)
            return sorted(items)

        def numbered(steps_and_kinds):
            seen, out = {}, []
            for step, kind in steps_and_kinds:
                out.append((step, kind, seen.get(kind, 0)))
                seen[kind] = seen.get(kind, 0) + 1
            return out

        def stream(img, opening):
            if opening:
                PROJ0, CHUNK0, ROW0 = 0, 0, 0
                items = numbered([(None, "project")] * TILES + [(None, "turn_g")] + [(None, "chunk")] * LEAD)
            else:
                PROJ0, CHUNK0, ROW0 = TILES, LEAD, 2
                items = numbered([(u * STEPS + step, kind) for u in range(PAIR) for step, kind in image_items()])
            at_step = {step: (n, kind, k) for n, (step, kind, k) in enumerate(items)}
            tiles = PAIR * TILES
            last_q = tiles * MB

            def half_of(kind, k):
                n = [(x, y) for _s, x, y in items].index((kind, k))
                return ps_scores[:, n % 2, :]

            def which(k):
                return (PROJ0 + k) // TILES % 2, (PROJ0 + k) % TILES

            with nc.Block() as block:
                @block.sync
                def _(sp):
                    def load_xt(k):
                        if k >= 4:
                            sp.wait_ge(s_xhi, k - 3)
                            sp.wait_ge(s_xlo_p, k - 3)
                        ahead, place = divmod(PROJ0 + k, TILES)
                        src = xT[(img + ahead) % B]
                        sp.dma_start(x_raw[:, k % 2, :, :], src[place]).then_inc(s_xt[k % 2], 16)

                    def load_xn(t):
                        if t >= 3:
                            sp.wait_ge(s_y, 2 * (t - 2))
                        sp.dma_start(x_nat[:, t % 3, :, :], xN[img * TILES + t]).then_inc(s_xn[t % 3], 16)

                    def store_y(t):
                        sp.wait_ge(s_y, 2 * (t + 1))
                        sp.dma_start(yN[img * TILES + t], y_val[:, t % 3, :, :]).then_inc(s_yst[t % 3], 16)

                    load_xt(2)
                    load_xt(3)
                    if opening:
                        for k in range(4, TILES + 2):
                            load_xt(k)
                        return
                    for t in range(3):
                        load_xn(t)
                    for q in range(last_q):
                        t, b = divmod(q, MB)
                        _n, kind, k = at_step.get(q - 4, (None, None, None))
                        if kind == "project" and k + 4 < tiles + 2:
                            load_xt(k + 4)
                        if b == 7 and t >= 1:
                            store_y(t - 1)
                            if t + 2 < tiles:
                                load_xn(t + 2)
                    store_y(tiles - 1)
                    for k in range(3):
                        sp.wait_ge(s_yst[k], 16 * len(range(k, tiles, 3)))

                @block.tensor
                def _(pe):
                    def half_free(n):
                        if n < 2:
                            return
                        _step, kind, k = items[n - 2]
                        if kind == "chunk":
                            pe.wait_ge(s_z, k + 1)
                        elif kind == "project":
                            pe.wait_ge(s_th_lo, k + 1)
                            pe.wait_ge(s_gpool, k + 1)
                        elif kind == "moments":
                            pe.wait_ge(s_momadd, k + 1)
                        else:
                            pe.wait_ge(s_gval, k + 1)

                    def project(acc2, k):
                        slot = k % 2
                        acc = acc2[:, 0:NT]
                        if k >= 2:
                            pe.wait_ge(s_xhi, k - 1)
                        for cc in range(CC):
                            pe.matmul(acc, w_tp_hi[:, cc, :], x_hi[:, slot, cc, :], start=(cc == 0), stop=False)
                            pe.matmul(acc, w_tp_lo[:, cc, :], x_hi[:, slot, cc, :], start=False, stop=False)
                        if k >= 2:
                            pe.wait_ge(s_xlo_p, k - 1)
                        for cc in range(CC):
                            last = pe.matmul(acc, w_tp_hi[:, cc, :], x_lo[:, slot, cc, :],
                                             start=False, stop=(cc == CC - 1))
                        last.then_inc(s_tp, 1)

                    def project_g(acc2, k):
                        slot = k % 2
                        acc = acc2[:, NT:2 * NT]
                        for cc in range(CC):
                            pe.matmul(acc, w_g_hi[:, cc, :], x_hi[:, slot, cc, :], start=(cc == 0), stop=False)
                            pe.matmul(acc, w_g_lo[:, cc, :], x_hi[:, slot, cc, :], start=False, stop=False)
                            last = pe.matmul(acc, w_g_hi[:, cc, :], x_lo[:, slot, cc, :],
                                             start=False, stop=(cc == CC - 1))
                        last.then_inc(s_g, 1)

                    def turn_g(acc, k):
                        pe.wait_ge(s_gpool, TILES * (k + 1))
                        for m in range(MB):
                            last = pe.transpose(acc[:, m * P:(m + 1) * P], g_pool[:, m, :], ident[:, :])
                        last.then_inc(s_gT, 1)

                    def scores(acc, k):
                        c = CHUNK0 + k
                        image, c_in = divmod(c, CHUNKS)
                        if c_in == 0:
                            done = TILES * (1 if opening else image)
                            pe.wait_ge(s_phi, 2 * done)
                            pe.wait_ge(s_philo, done)
                            pe.wait_ge(s_th_lo, done)
                        for h in range(2):
                            last = pe.matmul(acc[:, h * NT:(h + 1) * NT],
                                             theta[0:SHIFT, image % 2, c_in * P:(c_in + 1) * P],
                                             phi[0:SHIFT, image % 2, h * NT:(h + 1) * NT], start=True, stop=True)
                        last.then_inc(s_scores, 1)

                    def moments(acc, k):
                        t = 2 * (k - 1)
                        if k >= 1:
                            pe.wait_ge(s_yhi, t + 2)
                            pe.wait_ge(s_ylo, t + 2)
                        moments_of(pe, acc, t % Y_RING, True)

                    def moments_rest(acc, k):
                        t = 2 * (k - 1)
                        moments_of(pe, acc, (t + 1) % Y_RING, False).then_inc(s_mom, 1)

                    def item(n):
                        _step, kind, k = items[n]
                        half_free(n)
                        work = {"chunk": scores, "project": project, "moments": moments, "turn_g": turn_g}[kind]
                        work(ps_scores[:, n % 2, :], k)

                    def item_rest(n):
                        _step, kind, k = items[n]
                        if kind == "project":
                            project_g(ps_scores[:, n % 2, :], k)
                        elif kind == "moments":
                            moments_rest(ps_scores[:, n % 2, :], k)

                    def turn_max(t):
                        if NC * (t + 1) > CHUNK0:
                            pe.wait_ge(s_max, NC * (t + 1) - CHUNK0)
                        if t >= 3:
                            pe.wait_ge(s_y, 2 * (t - 2))
                        for j in range(NC):
                            last = pe.transpose(ps_oy[0:1, (t + 1) % 2, j * P:(j + 1) * P].bitcast(F32R),
                                                neg_max[:, t % TURNS, j:j + 1], ident_r[:, :])
                        last.then_inc(s_rowT, 1)

                    def scores_t(q):
                        t, b = divmod(q, MB)
                        if b == 0 and t >= 2:
                            pe.wait_ge(s_row, t - 1)
                        if q >= 2:
                            pe.wait_ge(s_e, q - 1)
                        u, place = t // TILES % 2, t % TILES
                        pe.matmul(ps_st[:, q % 2, :], phi[0:SHIFT + 1, u, b * P:(b + 1) * P],
                                  theta[0:SHIFT + 1, u, place * NT:(place + 1) * NT],
                                  start=True, stop=True).then_inc(s_st, 1)

                    def attend(q):
                        t, b = divmod(q, MB)
                        u = t // TILES % 2
                        acc = ps_oy[:, t % 2, :]
                        if b == 0 and t >= 1:
                            if t >= 2:
                                pe.wait_ge(s_y, 2 * (t - 1))
                            pe.wait_ge(s_row, t)
                        if b == 0 and t % TILES == 0 and t >= TILES:
                            pe.wait_ge(s_glo, t // TILES)
                        first, last = b == 0, b == MB - 1
                        if is_split(q):
                            e_slot = splits(q) % SPLIT_RING
                            pe.wait_ge(s_ehi, splits(q + 1))
                            pe.matmul(acc, g_hi[:, u, b, :], e_hi[:, e_slot, :], start=first, stop=False)
                            pe.matmul(acc, g_lo[:, u, b, :], e_hi[:, e_slot, :], start=False, stop=False)
                            if pool_takes(q):
                                pe.wait_ge(s_elo_p, pool_los(q + 1))
                            else:
                                pe.wait_ge(s_elo_v, dve_los(q + 1))
                            pe.matmul(acc, g_hi[:, u, b, :], e_lo[:, e_slot, :], start=False,
                                      stop=last).then_inc(s_av, 1)
                        else:
                            pe.wait_ge(s_e, q + 1)
                            pe.matmul(acc, g_val[:, u, b, :], e_val[:, q % RING, :], start=first,
                                      stop=last).then_inc(s_av, 1)

                    def project_out(t, half):
                        if half == 0:
                            pe.wait_ge(s_olo, t + 1)
                        else:
                            pe.wait_ge(s_y, 2 * t + 1)
                        for k in range(2):
                            cols = slice((2 * half + k) * P, (2 * half + k + 1) * P)
                            acc = ps_oy[:, t % 2, k * C:(k + 1) * C]
                            pe.matmul(acc, o_hi[:, t % 2, cols], w_o_hi[:, :], start=True, stop=False)
                            pe.matmul(acc, o_hi[:, t % 2, cols], w_o_lo[:, :], start=False, stop=False)
                            last = pe.matmul(acc, o_lo[:, t % 2, cols], w_o_hi[:, :], start=False, stop=True)
                        last.then_inc(s_yps, 1)

                    if opening:
                        for n in range(len(items)):
                            item(n)
                            item_rest(n)
                        turn_max(0)
                        turn_max(1)
                        return
                    for q in range(AHEAD):
                        scores_t(q)
                    for q in range(last_q):
                        t, b = divmod(q, MB)
                        if q + AHEAD < last_q:
                            scores_t(q + AHEAD)
                        if b in (2, 4) and t >= 1:
                            project_out(t - 1, b // 4)
                        attend(q)
                        if q in at_step:
                            item(at_step[q][0])
                        if q in at_step:
                            item_rest(at_step[q][0])
                        if b == 6:
                            turn_max(t + 2)
                    project_out(tiles - 1, 0)
                    project_out(tiles - 1, 1)

                @block.scalar
                def _(act):
                    def split_x(k):
                        act.wait_ge(s_xt[k % 2], 16 * (k // 2))
                        act.wait_ge(s_g, k - 1)
                        act.copy(x_hi[:, k % 2, :, :], x_raw[:, k % 2, :, :]).then_inc(s_xhi, 1)

                    def theta_hi(k):
                        buf, place = which(k)
                        act.wait_ge(s_tp, k + 1)
                        act.copy(theta[0:SHIFT, buf, place * NT:(place + 1) * NT],
                                 half_of("project", k)[0:SHIFT, 0:NT]).then_inc(s_th_hi, 1)

                    def stack_phi(k):
                        buf, place = which(k)
                        cols = slice(place * P, (place + 1) * P)
                        act.wait_ge(s_phipool, k + 1)
                        if k >= 2:
                            act.wait_ge(s_philo, k - 1)
                        act.copy(phi_hi[SHIFT:, k % 2, :], phi_pool[SHIFT:, k % 2, :]).then_inc(s_phihi, 1)
                        act.wait_ge(s_phihi, k + 1)
                        for m in range(2):
                            act.copy(phi[m * DA:(m + 1) * DA, buf, cols],
                                     phi_hi[SHIFT:, k % 2, :].bitcast(F32)).then_inc(s_phi, 1)

                    def copy_g(k):
                        act.wait_ge(s_gT, k + 1)
                        act.copy(g_val[:, which(k * TILES)[0], :, :].rearrange("p m d -> p (m d)"),
                                 half_of("turn_g", k)).then_inc(s_gval, 1)

                    def exp_sum(k):
                        t, j = divmod(CHUNK0 + k, NC)
                        act.wait_ge(s_max, k + 1)
                        if k >= 2:
                            act.wait_ge(s_z, k - 1)
                        act.activation(dump[:, k % 2, :], half_of("chunk", k), ACT.Exp,
                                       bias=neg_max[:, t % TURNS, j:j + 1].bitcast(F32),
                                       accum_out=total[:, t % TURNS, j:j + 1]).then_inc(s_z, 1)

                    def copy_row(t):
                        act.wait_ge(s_rowT, t + 1 - ROW0)
                        u, place = t // TILES % 2, t % TILES
                        act.copy(theta[SHIFT:SHIFT + 1, u, place * NT:(place + 1) * NT],
                                 ps_oy[0:1, (t + 1) % 2, :]).then_inc(s_row, 1)

                    def exponentiate(q):
                        act.wait_ge(s_st, q + 1)
                        if q >= RING:
                            act.wait_ge(s_av, q - RING + 1)
                        act.activation(e_val[:, q % RING, :], ps_st[:, q % 2, :], ACT.Exp).then_inc(s_e, 1)

                    def split_o(t):
                        act.wait_ge(s_av, MB * (t + 1))
                        if t >= 2:
                            act.wait_ge(s_yps, 2 * (t - 1))
                        act.copy(o_hi[:, t % 2, :], ps_oy[:, t % 2, :]).then_inc(s_ohi, 1)

                    if opening:
                        for k in range(TILES + 1):
                            if k >= 1:
                                theta_hi(k - 1)
                                split_x(k + 1)
                            if k >= 2:
                                stack_phi(k - 2)
                        stack_phi(TILES - 1)
                        copy_g(0)
                        for k in range(LEAD):
                            exp_sum(k)
                        copy_row(0)
                        copy_row(1)
                        return
                    for q in range(AHEAD):
                        exponentiate(q)
                    for q in range(last_q):
                        t, b = divmod(q, MB)
                        if b == 0 and t >= 1:
                            split_o(t - 1)
                        if b == 7:
                            copy_row(t + 2)
                        if q + AHEAD < last_q:
                            exponentiate(q + AHEAD)
                        for before in (1, 2, 3):
                            _n, kind, k = at_step.get(q - before, (None, None, None))
                            if kind == "chunk" and before == 1:
                                exp_sum(k)
                            elif kind == "turn_g" and before == 1:
                                copy_g(k)
                            elif kind == "project" and before == 1:
                                theta_hi(k)
                            elif kind == "project" and before == 2:
                                split_x(k + 2)
                            elif kind == "project" and before == 3:
                                stack_phi(k)
                    split_o(tiles - 1)

                @block.vector
                def _(dve):
                    def window(ap):
                        return ap.rearrange("p (r h w v) -> p r w h v", r=ROWS // 2, h=2, v=2)

                    def pooled(ap):
                        return ap.rearrange("p (r w) -> p r w", r=ROWS // 2)

                    def pool_phi(k):
                        dve.wait_ge(s_tp, k + 1)
                        if k >= 2:
                            dve.wait_ge(s_phihi, k - 1)
                            dve.wait_ge(s_philo, k - 1)
                        dve.tensor_reduce(pooled(phi_pool[SHIFT:, k % 2, :]),
                                          window(half_of("project", k)[SHIFT:, 0:NT]),
                                          AX.XY, ALU.max).then_inc(s_phipool, 1)

                    def pool_g(k):
                        dve.wait_ge(s_g, k + 1)
                        if k >= TILES:
                            dve.wait_ge(s_gT, k // TILES)
                        dve.tensor_reduce(pooled(g_pool[:, k % TILES, :]),
                                          window(half_of("project", k)[:, NT:2 * NT]),
                                          AX.XY, ALU.max).then_inc(s_gpool, 1)

                    def theta_lo(k):
                        buf, place = which(k)
                        dve.wait_ge(s_th_hi, k + 1)
                        dst = theta[DA:2 * DA, buf, place * NT:(place + 1) * NT]
                        dve.tensor_tensor(dst, half_of("project", k)[DA:2 * DA, 0:NT],
                                          dst.bitcast(F32), ALU.subtract).then_inc(s_th_lo, 1)

                    def phi_lo(k):
                        buf, place = which(k)
                        dve.wait_ge(s_phihi, k + 1)
                        dve.tensor_tensor(phi[2 * DA:3 * DA, buf, place * P:(place + 1) * P],
                                          phi_pool[SHIFT:, k % 2, :],
                                          phi_hi[SHIFT:, k % 2, :].bitcast(F32), ALU.subtract).then_inc(s_philo, 1)

                    def split_g(k):
                        buf = which(k * TILES)[0]
                        dve.wait_ge(s_gval, k + 1)
                        dve.tensor_copy(g_hi[:, buf, :, :], g_val[:, buf, :, :]).then_inc(s_ghi, 1)
                        dve.wait_ge(s_ghi, k + 1)
                        dve.tensor_tensor(g_lo[:, buf, :, :], g_val[:, buf, :, :],
                                          g_hi[:, buf, :, :].bitcast(F32), ALU.subtract).then_inc(s_glo, 1)

                    def maximum(k):
                        t, j = divmod(CHUNK0 + k, NC)
                        dve.wait_ge(s_scores, k + 1)
                        dve.tensor_reduce(neg_max[:, t % TURNS, j:j + 1], half_of("chunk", k), AX.X, ALU.max,
                                          negate=True).then_inc(s_max, 1)

                    def add_moments(k):
                        dve.wait_ge(s_mom, k + 1)
                        if k >= 1:
                            dve.wait_ge(s_momadd, k)
                        dve.tensor_tensor(moments_flat, half_of("moments", k)[:, 0:NT + UPPER], moments_flat,
                                          ALU.add).then_inc(s_momadd, 1)

                    def split_e_hi(q):
                        dve.wait_ge(s_e, q + 1)
                        used = split_before(q, SPLIT_RING)
                        if used is not None:
                            dve.wait_ge(s_av, used + 1)
                        dve.tensor_copy(e_hi[:, splits(q) % SPLIT_RING, :], e_val[:, q % RING, :]).then_inc(s_ehi, 1)

                    def split_e_lo(q):
                        dve.wait_ge(s_ehi, splits(q + 1))
                        dve.tensor_tensor(e_lo[:, splits(q) % SPLIT_RING, :], e_val[:, q % RING, :],
                                          e_hi[:, splits(q) % SPLIT_RING, :].bitcast(F32), ALU.subtract
                                          ).then_inc(s_elo_v, 1)

                    def split_o(t):
                        dve.wait_ge(s_ohi, t + 1)
                        dve.tensor_tensor(o_lo[:, t % 2, :], ps_oy[:, t % 2, :], o_hi[:, t % 2, :].bitcast(F32),
                                          ALU.subtract).then_inc(s_olo, 1)

                    def weight_scale(t):
                        if NC * (t + 1) > CHUNK0:
                            dve.wait_ge(s_z, NC * (t + 1) - CHUNK0)
                        dve.reciprocal(recip[:, t % 2, :], total[:, t % TURNS, :]).then_inc(s_recip, 1)
                        dve.wait_ge(s_recip, t + 1)
                        dve.tensor_scalar(scale[:, t % 2, :], recip[:, t % 2, :], sig[:, 0:1], None,
                                          ALU.mult).then_inc(s_scale, 1)

                    def residual(t, half):
                        if half == 0:
                            dve.wait_ge(s_scale, t + 1)
                            dve.wait_ge(s_xn[t % 3], 16 * (t // 3 + 1))
                            if t >= 3:
                                dve.wait_ge(s_yst[t % 3], 16 * (t // 3))
                                dve.wait_ge(s_ylo, t - 2)
                                dve.wait_ge(s_ysum, t - 2)
                        dve.wait_ge(s_yps, 2 * t + half + 1)
                        for k in range(2):
                            j = 2 * half + k
                            last = dve.scalar_tensor_tensor(y_val[:, t % 3, j, :], ps_oy[:, t % 2, k * C:(k + 1) * C],
                                                            scale[:, t % 2, j:j + 1], x_nat[:, t % 3, j, :],
                                                            ALU.mult, ALU.add)
                        last.then_inc(s_y, 1)

                    def split_y(t):
                        dve.wait_ge(s_y, 2 * (t + 1))
                        if t >= 2:
                            dve.wait_ge(s_mom, t // 2)
                        dve.tensor_copy(y_split[:, t % Y_RING, :, 0:C], y_val[:, t % 3, :, :]).then_inc(s_yhi, 1)

                    def split_y_lo(t):
                        dve.wait_ge(s_yhi, t + 1)
                        dve.wait_ge(s_ylo, t)
                        dve.tensor_tensor(y_split[:, t % Y_RING, :, C:], y_val[:, t % 3, :, :],
                                          y_split[:, t % Y_RING, :, 0:C].bitcast(F32), ALU.subtract
                                          ).then_inc(s_ylo, 1)

                    if opening:
                        for k in range(TILES + 1):
                            if k >= 1:
                                pool_phi(k - 1)
                                pool_g(k - 1)
                                theta_lo(k - 1)
                            if k >= 2:
                                phi_lo(k - 2)
                        phi_lo(TILES - 1)
                        for k in range(LEAD):
                            maximum(k)
                            if k == 1:
                                split_g(0)
                        return
                    for q in range(0, SPLIT_AHEAD):
                        if is_split(q):
                            split_e_hi(q)
                            if not pool_takes(q):
                                split_e_lo(q)
                    for q in range(last_q):
                        t, b = divmod(q, MB)
                        if b in (3, 5) and t >= 1:
                            residual(t - 1, b // 5)
                        if q + SPLIT_AHEAD < last_q and is_split(q + SPLIT_AHEAD):
                            split_e_hi(q + SPLIT_AHEAD)
                        if q + SPLIT_AHEAD < last_q and is_split(q + SPLIT_AHEAD) and not pool_takes(q + SPLIT_AHEAD):
                            split_e_lo(q + SPLIT_AHEAD)
                        if b == 6:
                            weight_scale(t)
                        if b == 7 and t >= 1:
                            split_y(t - 1)
                        if b == 0 and t >= 1:
                            split_o(t - 1)
                        for before in (1, 2, 4):
                            _n, kind, k = at_step.get(q - before, (None, None, None))
                            if kind == "chunk" and before == 1:
                                maximum(k)
                            elif kind == "moments" and before == 1:
                                add_moments(k)
                            elif kind == "turn_g" and before == 2:
                                split_g(k)
                            elif kind == "project" and before == 1:
                                pool_phi(k)
                                pool_g(k)
                                theta_lo(k)
                            elif kind == "project" and before == 4:
                                phi_lo(k)
                    split_o(tiles - 1)
                    residual(tiles - 1, 0)
                    residual(tiles - 1, 1)
                    split_y(tiles - 1)
                    split_y_lo(tiles - 1)

                @block.gpsimd
                def _(pool):
                    def split_x(k):
                        pool.wait_ge(s_xhi, k - 1)
                        pool.tensor_tensor(x_lo[:, k % 2, :, :], x_raw[:, k % 2, :, :],
                                           x_hi[:, k % 2, :, :].bitcast(F32), ALU.subtract).then_inc(s_xlo_p, 1)

                    def split_e(q):
                        pool.wait_ge(s_ehi, splits(q + 1))
                        pool.tensor_tensor(e_lo[:, splits(q) % SPLIT_RING, :], e_val[:, q % RING, :],
                                           e_hi[:, splits(q) % SPLIT_RING, :].bitcast(F32), ALU.subtract
                                           ).then_inc(s_elo_p, 1)

                    def sum_y(t):
                        pool.wait_ge(s_y, 2 * (t + 1))
                        if t >= 1:
                            pool.wait_ge(s_ysum, t)
                        pool.tensor_tensor(y_sum[:, :, :], y_sum[:, :, :], y_val[:, t % 3, :, :],
                                           ALU.add).then_inc(s_ysum, 1)

                    def split_y(t):
                        pool.wait_ge(s_yhi, t + 1)
                        pool.tensor_tensor(y_split[:, t % Y_RING, :, C:], y_val[:, t % 3, :, :],
                                           y_split[:, t % Y_RING, :, 0:C].bitcast(F32), ALU.subtract
                                           ).then_inc(s_ylo, 1)

                    if opening:
                        for k in range(2, TILES + 2):
                            split_x(k)
                        return
                    for q in range(last_q):
                        t, b = divmod(q, MB)
                        if b == 7 and t >= 1:
                            split_y(t - 1)
                        if b == 1 and t >= 2:
                            sum_y(t - 2)
                        if q + SPLIT_AHEAD < last_q and pool_takes(q + SPLIT_AHEAD):
                            split_e(q + SPLIT_AHEAD)
                        _n, kind, k = at_step.get(q - 3, (None, None, None))
                        if kind == "project":
                            split_x(k + 2)
                    sum_y(tiles - 2)
                    sum_y(tiles - 1)

            nc.all_engine_barrier(sems_to_clear=range(cleared[0].num, cleared[-1].num + 1))

        stream(0, True)
        with nc.Fori(0, B // PAIR) as pair:
            stream(pair * PAIR, False)

        s_rest = sem("s_rest")
        with nc.Block() as block:
            @block.tensor
            def _(pe):
                moments_of(pe, ps_scores[:, 0, :], Y_RING - 2, True)
                moments_of(pe, ps_scores[:, 0, :], Y_RING - 1, False).then_inc(s_rest, 1)

            @block.vector
            def _(dve):
                dve.wait_ge(s_rest, 1)
                dve.tensor_tensor(moments_flat, ps_scores[:, 0, 0:NT + UPPER], moments_flat,
                                  ALU.add).then_inc(s_rest, 1)

        row_s = sb("row_s", [1, C])
        mean = sb("mean", [P, CC])
        scratch = e_val[:, :, :].rearrange("p r n -> p (r n)").rearrange("p (k c) -> p k c", c=P)
        hl = scratch[:, 0:3, :]
        a_mat = scratch[:, 3:6, :]
        elim = e_val[:, :, :].rearrange("p r n -> p (r n)")[:, 6 * P:8 * P]
        diag = scratch[:, 8, :]
        w_inv = scratch[:, 9:11, :]
        w_invT = scratch[:, 11:13, :]
        b_mat = scratch[:, 13, :]
        x_mat = scratch[:, 14, :]
        w_10 = scratch[:, 15, :]
        wg = scratch[:, 16:19, :]
        wgT = scratch[:, 19:22, :]
        more = x_raw[:, :, :, :].rearrange("p s a n -> p (s a n)").rearrange("p (k c) -> p k c", c=P)
        schur = more[:, 0, :]
        above = more[:, 1, :]
        product = more[:, 3, :]
        step_T = more[:, 4, :]
        off = more[:, 5, :]
        rinv = sb("rinv", [P, 1])
        mult = sb("mult", [P, 1])
        dcol = sb("dcol", [P, 3])
        settled = sb("settled", [P, 3])
        settled_rows = sb("settled_rows", [1, 1], mybir.dt.int32)
        wgT_hi = theta[:, 0, 0:3 * P].rearrange("p (k c) -> p k c", k=3)
        wgT_lo = theta[:, 1, 0:3 * P].rearrange("p (k c) -> p k c", k=3)
        bias = sb("bias", [P, CC])

        covariance(nc, sem("s_cov"), y_sum, row_s, mean, hl, a_mat, moment, ident, ones,
                   ps_scores, ps_st, ps_oy, TOTAL)
        newton(nc, sem("s_newton"), a_mat, schur, above, below, ident, ones, product, step_T, off,
               dcol, settled, settled_rows, w_inv, w_invT, b_mat, x_mat, w_10, ps_scores, ps_st, ps_oy)
        nc.all_engine_barrier()
        rows = nc.values_load(settled_rows[0:1, 0:1], min_val=0, max_val=P,
                              skip_runtime_bounds_check_because="a count of partitions")
        with nc.If(rows < P):
            eliminate(nc, sem("s_elim"), a_mat, elim, diag, rinv, mult, dcol, below, ident,
                      w_inv, w_invT, b_mat, x_mat, w_10, ps_st, ps_oy)
        fold(nc, sem("s_fold"), w_inv, w_10, wg, wgT, wgT_hi, wgT_lo, gam, bet, mean, bias, ident, ps_st, ps_oy)

        whiten(nc, ctx, yN, outT, x_nat, y_val, ps_scores, ps_st, ps_oy, ident, wgT_hi, wgT_lo, bias,
               x_hi, x_lo, B * TILES, TILES)


def covariance(nc, s_f, y_sum, row_s, mean, hl, a_mat, moment, ident, ones, ps_scores, ps_st, ps_oy, total):
    C = row_s.shape[1]
    CC = C // P
    with nc.Block() as block:
        @block.tensor
        def _(pe):
            for j in range(NC):
                last = pe.matmul(ps_oy[0:1, 0, 0:C], ones[:, 0:1], y_sum[:, j, :], start=(j == 0), stop=(j == NC - 1))
            last.then_inc(s_f, 1)
            for a in range(CC):
                for j in range(NC):
                    last = pe.matmul(ps_oy[:, 1, a:a + 1], y_sum[:, j, a * P:(a + 1) * P], ones[:, 0:1],
                                     start=(j == 0), stop=(j == NC - 1))
            last.then_inc(s_f, 1)
            pe.wait_ge(s_f, 4)
            for a in range(CC):
                last = pe.matmul(ps_st[:, a, 0:C], row_s[0:1, a * P:(a + 1) * P], row_s[0:1, :],
                                 start=True, stop=True)
            last.then_inc(s_f, 1)
            pe.wait_ge(s_f, 8)
            for k in range(3):
                last = pe.transpose(ps_scores[:, 0, k * P:(k + 1) * P], hl[:, k, :], ident[:, :])
            last.then_inc(s_f, 1)

        @block.vector
        def _(dve):
            dve.wait_ge(s_f, 2)
            dve.tensor_copy(row_s[0:1, :], ps_oy[0:1, 0, 0:C]).then_inc(s_f, 1)
            dve.tensor_scalar(mean[:, :], ps_oy[:, 1, 0:CC], 1.0 / total, None, ALU.mult).then_inc(s_f, 1)
            dve.wait_ge(s_f, 5)
            for k, (a, col) in enumerate(((0, 2 * P), (1, P), (1, 2 * P))):
                dve.tensor_copy(hl[:, k, :], moment[:, a, col:col + P]).then_inc(s_f, 1)
            dve.wait_ge(s_f, 9)
            blocks = ((moment[:, 0, 0:P], hl[:, 0, :], ps_st[:, 0, 0:P]),
                      (moment[:, 0, P:2 * P], moment[:, 0, 3 * P:4 * P], ps_st[:, 0, P:2 * P]),
                      (moment[:, 1, 0:P], hl[:, 2, :], ps_st[:, 1, P:2 * P]))
            n = 9
            for k, (hh, own, outer) in enumerate(blocks):
                dst = a_mat[:, k, :]
                dve.tensor_copy(dst, hh).then_inc(s_f, 1)
                dve.wait_ge(s_f, n + 1)
                dve.tensor_tensor(dst, own, dst, ALU.add).then_inc(s_f, 1)
                dve.wait_ge(s_f, n + 2)
                dve.tensor_tensor(dst, ps_scores[:, 0, k * P:(k + 1) * P], dst, ALU.add).then_inc(s_f, 1)
                dve.wait_ge(s_f, n + 3)
                dve.scalar_tensor_tensor(dst, outer, -1.0 / total, dst, ALU.mult, ALU.add).then_inc(s_f, 1)
                dve.wait_ge(s_f, n + 4)
                dve.tensor_scalar(dst, dst, (1.0 - WHITEN_EPS) / (total - 1.0), None, ALU.mult).then_inc(s_f, 1)
                n += 5
                if k != 1:
                    dve.wait_ge(s_f, n)
                    dve.scalar_tensor_tensor(dst, ident[:, :], WHITEN_EPS, dst, ALU.mult, ALU.add).then_inc(s_f, 1)
                    n += 1


def newton(nc, s_f, a_mat, schur, above, below, ident, ones, product, step_T, off, dcol, settled,
           settled_rows, w_inv, w_invT, b_mat, x_mat, w_10, ps_scores, ps_st, ps_oy):
    MASK, START, TURN, CHECK, BETWEEN = 2, 6, 7, 4, 5
    first = (MASK, MASK + START + TURN * NEWTON_STEPS + CHECK + BETWEEN)
    checked = [f + START + TURN * NEWTON_STEPS + CHECK for f in first]

    with nc.Block() as block:
        @block.tensor
        def _(pe):
            def after(n):
                pe.wait_ge(s_f, n)

            pe.transpose(ps_oy[:, 0, 0:P], below[:, :], ident[:, :]).then_inc(s_f, 1)
            for half in range(2):
                a = a_mat[:, 0, :] if half == 0 else schur
                w, wT = w_inv[:, half, :], w_invT[:, half, :]
                for i in range(NEWTON_STEPS):
                    base = first[half] + START + TURN * i
                    after(base)
                    pe.matmul(ps_st[:, 0, 0:P], a, wT, start=True, stop=True).then_inc(s_f, 1)
                    after(base + 2)
                    pe.matmul(ps_st[:, 1, 0:P], wT, product, start=True, stop=True).then_inc(s_f, 1)
                    after(base + 4)
                    pe.matmul(ps_oy[:, 0, 0:P], step_T, w, start=True, stop=True)
                    pe.matmul(ps_oy[:, 1, 0:P], w, step_T, start=True, stop=True).then_inc(s_f, 1)
                after(checked[half])
                if half == 0:
                    pe.matmul(ps_scores[:, 0, 0:P], wT, a_mat[:, 1, :], start=True, stop=True).then_inc(s_f, 1)
                    after(checked[0] + 2)
                    pe.matmul(ps_scores[:, 1, 0:P], b_mat[:, :], b_mat[:, :], start=True, stop=True)
                    pe.matmul(ps_scores[:, 1, P:2 * P], b_mat[:, :], w, start=True,
                              stop=True).then_inc(s_f, 1)
                else:
                    pe.matmul(ps_scores[:, 0, 0:P], wT, x_mat[:, :], start=True, stop=True)
                    pe.matmul(ps_scores[0:1, 1, 0:1], settled[:, 2:3], ones[:, 0:1], start=True,
                              stop=True).then_inc(s_f, 1)

        @block.vector
        def _(dve):
            n = [1]

            def step(ins):
                ins.then_inc(s_f, 1)
                n[0] += 1

            def others(count=1):
                n[0] += count

            def now():
                dve.wait_ge(s_f, n[0])

            now()
            step(dve.scalar_tensor_tensor(above, ident[:, :], -0.5, ps_oy[:, 0, 0:P], ALU.mult, ALU.add))
            for half in range(2):
                a = a_mat[:, 0, :] if half == 0 else schur
                w, wT = w_inv[:, half, :], w_invT[:, half, :]
                assert n[0] == first[half]
                step(dve.tensor_tensor(off, a, ident[:, :], ALU.mult))
                now()
                step(dve.tensor_reduce(dcol[:, 0:1], off, AX.X, ALU.add))
                now()
                step(dve.reciprocal(dcol[:, 1:2], dcol[:, 0:1]))
                others()
                now()
                step(dve.tensor_scalar(w, ident[:, :], dcol[:, 2:3], None, ALU.mult))
                step(dve.tensor_scalar(wT, ident[:, :], dcol[:, 2:3], None, ALU.mult))
                for i in range(NEWTON_STEPS):
                    assert n[0] == first[half] + START + TURN * i
                    others()
                    now()
                    step(dve.tensor_copy(product, ps_st[:, 0, 0:P]))
                    others()
                    now()
                    step(dve.tensor_tensor(step_T, ps_st[:, 1, 0:P], above, ALU.mult))
                    others()
                    now()
                    step(dve.scalar_tensor_tensor(w, w, 1.5, ps_oy[:, 0, 0:P], ALU.mult, ALU.add))
                    step(dve.scalar_tensor_tensor(wT, wT, 1.5, ps_oy[:, 1, 0:P], ALU.mult, ALU.add))
                step(dve.tensor_tensor(off, ps_st[:, 1, 0:P], ident[:, :], ALU.subtract))
                now()
                step(dve.tensor_tensor(off, off, off, ALU.mult))
                now()
                step(dve.tensor_reduce(dcol[:, 0:1], off, AX.X, ALU.add))
                now()
                if half == 0:
                    step(dve.tensor_scalar(settled[:, 0:1], dcol[:, 0:1], SETTLED, None, ALU.is_le))
                    assert n[0] == checked[0]
                    others()
                    now()
                    step(dve.tensor_copy(b_mat[:, :], ps_scores[:, 0, 0:P]))
                    others()
                    now()
                    step(dve.tensor_copy(x_mat[:, :], ps_scores[:, 1, P:2 * P]))
                    step(dve.scalar_tensor_tensor(schur, ps_scores[:, 1, 0:P], -1.0, a_mat[:, 2, :],
                                                  ALU.mult, ALU.add))
                    now()
                else:
                    step(dve.scalar_tensor_tensor(settled[:, 2:3], dcol[:, 0:1], SETTLED, settled[:, 0:1],
                                                  ALU.is_le, ALU.mult))
                    assert n[0] == checked[1]
                    others()
                    now()
                    step(dve.tensor_scalar(w_10[:, :], ps_scores[:, 0, 0:P], -1.0, None, ALU.mult))
                    step(dve.tensor_copy(settled_rows[0:1, 0:1], ps_scores[0:1, 1, 0:1]))

        @block.scalar
        def _(act):
            for half in range(2):
                act.wait_ge(s_f, first[half] + 3)
                act.activation(dcol[:, 2:3], dcol[:, 1:2], ACT.Sqrt).then_inc(s_f, 1)


def eliminate(nc, s_f, a_mat, elim, diag, rinv, mult, dcol, below, ident, w_inv, w_invT, b_mat, x_mat, w_10,
              ps_st, ps_oy):
    PIVOT, ROOT, BETWEEN = 4, 5, 7
    first = (0, 2 + PIVOT * P + ROOT + BETWEEN)
    rooted = [f + 2 + PIVOT * P + ROOT for f in first]

    with nc.Block() as block:
        @block.tensor
        def _(pe):
            def after(n):
                pe.wait_ge(s_f, n)

            for half in range(2):
                for k in range(P):
                    after(first[half] + 2 + PIVOT * k)
                    pe.matmul(ps_st[:, k % 2, 0:P + 1], ident[:, k:k + 1].to_broadcast([P, P]),
                              elim[:, k:k + P + 1], start=True, stop=True).then_inc(s_f, 1)
                after(rooted[half])
                pe.transpose(ps_oy[:, 0, 0:P], w_inv[:, half, :], ident[:, :]).then_inc(s_f, 1)
                after(rooted[half] + 2)
                if half == 0:
                    pe.matmul(ps_oy[:, 0, P:2 * P], w_invT[:, 0, :], a_mat[:, 1, :], start=True,
                              stop=True).then_inc(s_f, 1)
                    after(rooted[0] + 4)
                    pe.matmul(ps_oy[:, 1, 0:P], b_mat[:, :], b_mat[:, :], start=True, stop=True)
                    pe.matmul(ps_oy[:, 1, P:2 * P], b_mat[:, :], w_inv[:, 0, :], start=True,
                              stop=True).then_inc(s_f, 1)
                else:
                    pe.matmul(ps_oy[:, 0, P:2 * P], w_invT[:, 1, :], x_mat[:, :], start=True,
                              stop=True).then_inc(s_f, 1)

        @block.vector
        def _(dve):
            n = [0]

            def step(ins):
                ins.then_inc(s_f, 1)
                n[0] += 1

            def now():
                dve.wait_ge(s_f, n[0])

            def other():
                n[0] += 1
                now()

            for half in range(2):
                src = a_mat[:, 0, :] if half == 0 else a_mat[:, 2, :]
                assert n[0] == first[half]
                step(dve.tensor_copy(elim[:, 0:P], src))
                step(dve.tensor_copy(elim[:, P:], ident[:, :]))
                for k in range(P):
                    other()
                    row = ps_st[:, k % 2, 0:P + 1]
                    step(dve.reciprocal(rinv[:, :], row[:, 0:1]))
                    now()
                    step(dve.scalar_tensor_tensor(mult[:, :], elim[:, k:k + 1], below[:, k:k + 1], rinv[:, :],
                                                  ALU.mult, ALU.mult))
                    now()
                    cols = elim[:, k:k + P + 1]
                    step(dve.scalar_tensor_tensor(cols, row, mult[:, 0:1], cols, ALU.mult, ALU.add))
                now()
                step(dve.tensor_tensor(diag[:, :], elim[:, 0:P], ident[:, :], ALU.mult))
                now()
                step(dve.tensor_reduce(dcol[:, 0:1], diag[:, :], AX.X, ALU.add))
                now()
                step(dve.reciprocal(dcol[:, 1:2], dcol[:, 0:1]))
                other()
                step(dve.tensor_scalar(w_inv[:, half, :], elim[:, P:], mult[:, 0:1], None, ALU.mult))
                assert n[0] == rooted[half]
                other()
                step(dve.tensor_copy(w_invT[:, half, :], ps_oy[:, 0, 0:P]))
                other()
                if half == 0:
                    step(dve.tensor_copy(b_mat[:, :], ps_oy[:, 0, P:2 * P]))
                    other()
                    step(dve.tensor_copy(x_mat[:, :], ps_oy[:, 1, P:2 * P]))
                    step(dve.scalar_tensor_tensor(a_mat[:, 2, :], ps_oy[:, 1, 0:P], -1.0, a_mat[:, 2, :],
                                                  ALU.mult, ALU.add))
                    now()
                else:
                    step(dve.tensor_scalar(w_10[:, :], ps_oy[:, 0, P:2 * P], -1.0, None, ALU.mult))

        @block.scalar
        def _(act):
            for half in range(2):
                act.wait_ge(s_f, rooted[half] - 2)
                act.activation(mult[:, :], dcol[:, 1:2], ACT.Sqrt).then_inc(s_f, 1)

        @block.sync
        def _(sp):
            sp.wait_ge(s_f, rooted[1])

        @block.gpsimd
        def _(pool):
            pool.wait_ge(s_f, rooted[1])


def fold(nc, s_f, w_inv, w_10, wg, wgT, wgT_hi, wgT_lo, gam, bet, mean, bias, ident, ps_st, ps_oy):
    with nc.Block() as block:
        @block.vector
        def _(dve):
            dve.tensor_scalar(wg[:, 0, :], w_inv[:, 0, :], gam[:, 0:1], None, ALU.mult).then_inc(s_f, 1)
            dve.tensor_scalar(wg[:, 1, :], w_10[:, :], gam[:, 1:2], None, ALU.mult).then_inc(s_f, 1)
            dve.tensor_scalar(wg[:, 2, :], w_inv[:, 1, :], gam[:, 1:2], None, ALU.mult).then_inc(s_f, 1)
            dve.wait_ge(s_f, 4)
            dve.tensor_copy(wgT[:, :, :], ps_st[:, 0, 0:3 * P].rearrange("p (k c) -> p k c", k=3)).then_inc(s_f, 1)
            dve.wait_ge(s_f, 5)
            dve.tensor_copy(wgT_hi[:, :, :], wgT[:, :, :]).then_inc(s_f, 1)
            dve.wait_ge(s_f, 6)
            dve.tensor_tensor(wgT_lo[:, :, :], wgT[:, :, :], wgT_hi[:, :, :].bitcast(F32), ALU.subtract
                              ).then_inc(s_f, 1)
            dve.wait_ge(s_f, 8)
            dve.scalar_tensor_tensor(bias[:, :], ps_oy[:, 1, 0:2], -1.0, bet[:, :], ALU.mult, ALU.add
                                     ).then_inc(s_f, 1)

        @block.tensor
        def _(pe):
            pe.wait_ge(s_f, 3)
            for k in range(3):
                last = pe.transpose(ps_st[:, 0, k * P:(k + 1) * P], wg[:, k, :], ident[:, :])
            last.then_inc(s_f, 1)
            pe.wait_ge(s_f, 7)
            pe.matmul(ps_oy[:, 1, 0:1], wgT[:, 0, :], mean[:, 0:1], start=True, stop=True)
            pe.matmul(ps_oy[:, 1, 1:2], wgT[:, 1, :], mean[:, 0:1], start=True, stop=False)
            pe.matmul(ps_oy[:, 1, 1:2], wgT[:, 2, :], mean[:, 1:2], start=False, stop=True).then_inc(s_f, 1)


def whiten(nc, ctx, yN, outT, y_in, y_val, ps_scores, ps_st, ps_oy, ident, w_hi, w_lo, bias,
           yT_hi, yT_lo, tiles, per_image):
    C = yN.shape[3]
    CC = C // P

    def sem(name):
        return ctx.enter_context(nc.semaphore(name))

    out_sb = y_val[:, 0:2, :, :].rearrange("p s j c -> p s (j c)").rearrange("p s (a n) -> p s a n", a=CC)
    s_in = [sem("w_in0"), sem("w_in1")]
    s_turn = sem("w_turn")
    s_hi, s_lo = sem("w_hi"), sem("w_lo")
    s_mm = sem("w_mm")
    s_outa, s_outv = sem("w_outa"), sem("w_outv")
    s_st = [sem("w_st0"), sem("w_st1")]
    turned = [ps_scores[:, k, :].rearrange("p (a n) -> p a n", a=CC) for k in range(2)]
    prod = ((ps_st[:, 0, :], ps_st[:, 1, :]), (ps_oy[:, 0, :], ps_oy[:, 1, :]))

    with nc.Block() as block:
        @block.sync
        def _(sp):
            pairs = yN.rearrange("(u s) p j c -> u s p j c", s=2)

            def load(pair, slot):
                sp.dma_start(y_in[:, slot, :, :], pairs[pair, slot]).then_inc(s_in[slot], 16)

            load(0, 0)
            load(0, 1)
            with sp.Fori(1, tiles // 2) as u:
                for slot in range(2):
                    sp.wait_ge(s_turn, 2 * u - 1 + slot)
                    load(u, slot)

        @block.gpsimd
        def _(pool):
            with pool.Fori(0, tiles // per_image) as img:
                for k in range(per_image):
                    pool.wait_ge(s_outa, img * per_image + k + 1)
                    pool.wait_ge(s_outv, img * per_image + k + 1)
                    pool.dma_start(outT[img, k], out_sb[:, k % 2, :, :]).then_inc(s_st[k % 2], 16)
            for slot in range(2):
                pool.wait_ge(s_st[slot], 16 * (tiles // 2))

        @block.tensor
        def _(pe):
            def turn(slot, landed, free):
                pe.wait_ge(s_in[slot], landed)
                if free is not None:
                    pe.wait_ge(s_lo, free)
                for a in range(CC):
                    for j in range(NC):
                        last = pe.transpose(turned[slot][:, a, j * P:(j + 1) * P],
                                            y_in[:, slot, j, a * P:(a + 1) * P], ident[:, :])
                last.then_inc(s_turn, 1)

            def product(slot, split, free):
                if free is not None:
                    pe.wait_ge(s_outa, free)
                    pe.wait_ge(s_outv, free)
                pe.wait_ge(s_lo, split)
                blocks = (((0, 0),), ((1, 0), (2, 1)))
                for a in range(CC):
                    dst = prod[slot][a]
                    for k, (w, h) in enumerate(blocks[a]):
                        hi, lo = yT_hi[:, slot, h, :], yT_lo[:, slot, h, :]
                        pe.matmul(dst, w_hi[:, w, :], hi, start=(k == 0), stop=False)
                        pe.matmul(dst, w_hi[:, w, :], lo, start=False, stop=False)
                        last = pe.matmul(dst, w_lo[:, w, :], hi, start=False, stop=(k == len(blocks[a]) - 1))
                last.then_inc(s_mm, 1)

            turn(0, 16, None)
            turn(1, 16, None)
            product(0, 1, None)
            turn(0, 32, 1)
            product(1, 2, None)
            turn(1, 32, 2)
            product(0, 3, 1)
            with pe.Fori(4, tiles, 2) as i:
                turn(0, i * 8 + 16, i - 1)
                product(1, i, i - 2)
                turn(1, i * 8 + 16, i)
                product(0, i + 1, i - 1)
            product(1, tiles, tiles - 2)

        @block.scalar
        def _(act):
            def split(slot, turns, used):
                act.wait_ge(s_turn, turns)
                if used is not None:
                    act.wait_ge(s_mm, used)
                act.copy(yT_hi[:, slot, :, :], turned[slot]).then_inc(s_hi, 1)

            def finish(slot, products, stored):
                act.wait_ge(s_mm, products)
                if stored is not None:
                    act.wait_ge(s_st[slot], stored)
                act.activation(out_sb[:, slot, 0, :], prod[slot][0], ACT.Identity,
                               bias=bias[:, 0:1]).then_inc(s_outa, 1)

            split(0, 1, None)
            split(1, 2, None)
            finish(0, 1, None)
            split(0, 3, 1)
            finish(1, 2, None)
            split(1, 4, 2)
            finish(0, 3, 16)
            with act.Fori(4, tiles, 2) as i:
                split(0, i + 1, i - 1)
                finish(1, i, i * 8 - 16)
                split(1, i + 2, i)
                finish(0, i + 1, i * 8)
            finish(1, tiles, 8 * tiles - 16)

        @block.vector
        def _(dve):
            def split(slot, his, used):
                dve.wait_ge(s_hi, his)
                if used is not None:
                    dve.wait_ge(s_mm, used)
                dve.tensor_tensor(yT_lo[:, slot, :, :], turned[slot], yT_hi[:, slot, :, :].bitcast(F32),
                                  ALU.subtract).then_inc(s_lo, 1)

            def finish(slot, products, stored):
                dve.wait_ge(s_mm, products)
                if stored is not None:
                    dve.wait_ge(s_st[slot], stored)
                dve.tensor_scalar(out_sb[:, slot, 1, :], prod[slot][1], bias[:, 1:2], None,
                                  ALU.add).then_inc(s_outv, 1)

            split(0, 1, None)
            split(1, 2, None)
            finish(0, 1, None)
            split(0, 3, 1)
            finish(1, 2, None)
            split(1, 4, 2)
            finish(0, 3, 16)
            with dve.Fori(4, tiles, 2) as i:
                split(0, i + 1, i - 1)
                finish(1, i, i * 8 - 16)
                split(1, i + 2, i)
                finish(0, i + 1, i * 8)
            finish(1, tiles, 8 * tiles - 16)


def kernel(**inputs):
    import numpy as np
    import concourse.bacc as bacc
    from concourse.bass_utils import run_bass_kernel_spmd

    x = np.asarray(inputs["x"])
    B, H, W, C = x.shape
    N = H * W
    TILES, CC = N // NT, C // P
    flat = x.reshape(B, N, C)
    arrays = {
        "xT": np.ascontiguousarray(flat.reshape(B, TILES, NT, CC, P).transpose(0, 1, 4, 3, 2)),
        "xN": np.ascontiguousarray(flat.reshape(B * TILES, NT // P, P, C).transpose(0, 2, 1, 3)),
        "w_theta": np.asarray(inputs["L0_conv_w_theta"]),
        "w_phi": np.asarray(inputs["L0_conv_w_phi"]),
        "w_g": np.asarray(inputs["L0_conv_w_g"]),
        "w_out": np.asarray(inputs["L0_conv_w_out"]),
        "sigma": np.asarray(inputs["L0_conv_sigma"]).reshape(1),
        "gamma": np.asarray(inputs["L1_conv_gamma"]),
        "beta": np.asarray(inputs["L1_conv_beta"]),
    }
    nc = bacc.Bacc("TRN2", target_bir_lowering=False, num_devices=1)
    args = [nc.dram_tensor(f"in_{k}", a.shape, mybir.dt.from_np(a.dtype), kind="ExternalInput").ap()
            for k, a in arrays.items()]
    outT = nc.dram_tensor("out", [B, TILES, P, CC, NT], F32, kind="ExternalOutput").ap()
    attention_whitening_kernel(nc, *args, outT)
    r = run_bass_kernel_spmd(nc, [{f"in_{k}": a for k, a in arrays.items()}], core_ids=[0])
    got = r.results[0]["out"]
    return np.ascontiguousarray(got.reshape(B, TILES, P, CC, NT).transpose(0, 1, 4, 3, 2)).reshape(B, H, W, C)
```

```python
from contextlib import ExitStack

import concourse.bass as bass
from concourse import mybir

F32 = mybir.dt.float32
F32R = mybir.dt.float32r
ALU = mybir.AluOpType
ACT = mybir.ActivationFunctionType
AX = mybir.AxisListType

P = 128
NT = 512
NC = NT // P
WHITEN_EPS = 1e-3
NEWTON_STEPS = 4
SETTLED = 1e-9


def attention_whitening_kernel(nc, xT, xN, w_theta, w_phi, w_g, w_out, sigma, gamma, beta, outT):
    B, TILES, _P, CC, _NT = xT.shape
    C, N = CC * P, TILES * NT
    DA = w_theta.shape[1]
    DG = w_g.shape[1]
    WIDTH = 64
    ROWS = NT // WIDTH
    M = N // 4
    MB = M // P
    assert MB == TILES and DG == P and 3 * DA + DA == P
    TOTAL = B * N
    SHIFT = 3 * DA
    STEPS = TILES * MB
    GROUP = 2
    CHUNKS = TILES * NC
    RING = 6
    SPLIT_RING = 3
    AHEAD = 5
    SPLIT_AHEAD = 3
    LEAD = 9
    CHUNK_STEPS = range(0, STEPS, STEPS // CHUNKS)
    PROJ_STEPS = (1, 7, 11, 17, 21, 27, 31, 37)
    MOMENT_STEPS = (13, 29, 45, 57)
    TURN_STEP = 51
    Y_RING = 4
    TURNS = 4
    UPPER = 2 * C - P
    SETUP_LOADS = 5 + 2 * CC

    yN = nc.dram_tensor("y_spill", [B * TILES, P, NC, C], F32, kind="Internal").ap()

    with ExitStack() as ctx:
        def sb(name, shape, dt=F32):
            return ctx.enter_context(nc.sbuf_tensor(name, shape, dt))

        def ps(name, shape):
            return ctx.enter_context(nc.psum_tensor(name, shape, F32))

        def sem(name):
            return ctx.enter_context(nc.semaphore(name))

        ps_scores = ps("ps_scores", [P, 2, M])
        ps_st = ps("ps_st", [P, 2, NT])
        ps_oy = ps("ps_oy", [P, 2, NT])

        w_t = sb("w_t", [P, CC, DA])
        w_p = sb("w_p", [P, CC, DA])
        w_tp_hi = sb("w_tp_hi", [P, CC, P], F32R)
        w_tp_lo = sb("w_tp_lo", [P, CC, P], F32R)
        w_gs = sb("w_gs", [P, CC, DG])
        w_g_hi = sb("w_g_hi", [P, CC, DG], F32R)
        w_g_lo = sb("w_g_lo", [P, CC, DG], F32R)
        w_o = sb("w_o", [P, C])
        w_o_hi = sb("w_o_hi", [P, C], F32R)
        w_o_lo = sb("w_o_lo", [P, C], F32R)
        sig = sb("sig", [P, 1])
        gam = sb("gam", [P, CC])
        bet = sb("bet", [P, CC])
        ident = sb("ident", [P, P])
        ident_r = sb("ident_r", [P, P], F32R)
        ones = sb("ones", [P, P])
        below = sb("below", [P, P])
        moment = sb("moment", [P, 2, NT])

        x_raw = sb("x_raw", [P, 2, CC, NT])
        x_hi = sb("x_hi", [P, 2, CC, NT], F32R)
        x_lo = sb("x_lo", [P, 2, CC, NT], F32R)
        theta = sb("theta", [P, 2, N], F32R)
        phi = sb("phi", [P, 2, M], F32R)
        phi_pool = sb("phi_pool", [P, 2, P])
        phi_hi = sb("phi_hi", [P, 2, P], F32R)
        g_pool = sb("g_pool", [P, MB, P])
        g_val = sb("g_val", [P, 2, MB, DG])
        g_hi = sb("g_hi", [P, 2, MB, DG], F32R)
        g_lo = sb("g_lo", [P, 2, MB, DG], F32R)
        neg_max = sb("neg_max", [P, TURNS, NC], F32R)
        total = sb("total", [P, TURNS, NC])
        scale = sb("scale", [P, 2, NC])
        recip = sb("recip", [P, 2, NC])
        dump = sb("dump", [P, 2, M], mybir.dt.bfloat16)
        e_val = sb("e_val", [P, RING, NT])
        e_hi = sb("e_hi", [P, SPLIT_RING, NT], F32R)
        e_lo = sb("e_lo", [P, SPLIT_RING, NT], F32R)
        o_hi = sb("o_hi", [P, 2, NT], F32R)
        o_lo = sb("o_lo", [P, 2, NT], F32R)
        x_nat = sb("x_nat", [P, 3, NC, C])
        y_val = sb("y_val", [P, 3, NC, C])
        y_split = sb("y_split", [P, Y_RING, NC, 2 * C], F32R)
        y_sum = sb("y_sum", [P, NC, C])

        moments_flat = moment[:, :, :].rearrange("p a n -> p (a n)")[:, 0:NT + UPPER]

        s_setup_dma = sem("s_setup_dma")
        s_const0 = sem("s_const0")
        s_const = sem("s_const")
        s_whi = sem("s_whi")
        s_wlo = sem("s_wlo")
        s_first = sem("s_first")
        s_first_hi = sem("s_first_hi")
        s_first_lo = sem("s_first_lo")
        cleared = []

        def isem(name):
            s = sem(name)
            cleared.append(s)
            return s

        s_xt = [isem("s_xt0"), isem("s_xt1")]
        s_xhi = isem("s_xhi")
        s_xlo = isem("s_xlo")
        s_tp = isem("s_tp")
        s_g = isem("s_g")
        s_th_hi = isem("s_th_hi")
        s_th_lo = isem("s_th_lo")
        s_phipool = isem("s_phipool")
        s_gpool = isem("s_gpool")
        s_gT = isem("s_gT")
        s_ghi = isem("s_ghi")
        s_glo = isem("s_glo")
        s_phihi = isem("s_phihi")
        s_phi = isem("s_phi")
        s_philo = isem("s_philo")
        s_scores = isem("s_scores")
        s_max = isem("s_max")
        s_z = isem("s_z")
        s_rowT = isem("s_rowT")
        s_row = isem("s_row")
        s_st = isem("s_st")
        s_e = isem("s_e")
        s_ehi = isem("s_ehi")
        s_elo_v = isem("s_elo_v")
        s_elo_p = isem("s_elo_p")
        s_av = isem("s_av")
        s_ohi = isem("s_ohi")
        s_olo = isem("s_olo")
        s_yps = isem("s_yps")
        s_recip = isem("s_recip")
        s_scale = isem("s_scale")
        s_y = isem("s_y")
        s_yhi = isem("s_yhi")
        s_ylo = isem("s_ylo")
        s_ysum = isem("s_ysum")
        s_mom = isem("s_mom")
        s_momadd = isem("s_momadd")
        s_gval = isem("s_gval")
        s_xn = [isem(f"s_xn{k}") for k in range(3)]
        s_yst = [isem(f"s_yst{k}") for k in range(3)]

        with nc.Block() as block:
            @block.sync
            def _(sp):
                for dst, src in ((w_t, w_theta), (w_p, w_phi), (w_gs, w_g)):
                    sp.dma_start(dst[:, :, :], src.rearrange("(a p) d -> p a d", p=P)).then_inc(s_setup_dma, 16)
                for t in range(2):
                    sp.dma_start(x_raw[:, t, :, :], xT[0, t]).then_inc(s_first, 16)
                sp.dma_start(w_o[:, :], w_out).then_inc(s_setup_dma, 16)
                sp.dma_start(sig[:, :], sigma.partition_broadcast(P)).then_inc(s_setup_dma, 16)
                for dst, src in ((gam, gamma), (bet, beta)):
                    for a in range(CC):
                        sp.dma_start(dst[:, a:a + 1],
                                     src[a * P:(a + 1) * P].rearrange("(p o) -> p o", o=1)).then_inc(s_setup_dma, 16)
                sp.wait_ge(s_setup_dma, 16 * SETUP_LOADS)

            @block.gpsimd
            def _(pool):
                pool.memset(ident[:, :], 0.0).then_inc(s_const0, 1)
                pool.memset(below[:, :], 0.0).then_inc(s_const0, 1)
                pool.memset(ones[:, :], 1.0).then_inc(s_const, 1)
                pool.memset(y_sum[:, :, :], 0.0).then_inc(s_const, 1)
                pool.memset(moment[:, :, :], 0.0).then_inc(s_const, 1)
                pool.wait_ge(s_const0, 2)
                pool.affine_select(out=ident[:, :], in_=ident[:, :], compare_op=ALU.not_equal, fill=1.0,
                                   base=0, pattern=[[-1, P]], channel_multiplier=1).then_inc(s_const, 1)
                pool.affine_select(out=below[:, :], in_=below[:, :], compare_op=ALU.is_ge, fill=-1.0,
                                   base=0, pattern=[[1, P]], channel_multiplier=-1).then_inc(s_const, 1)

            @block.vector
            def _(dve):
                dve.memset(y_split[:, Y_RING - 2:, :, :].bitcast(F32), 0.0).then_inc(s_const, 1)
                dve.wait_ge(s_const, 6)
                dve.tensor_copy(ident_r[:, :], ident[:, :]).then_inc(s_const, 1)
                for buf in range(2):
                    dve.tensor_copy(phi[SHIFT:SHIFT + 1, buf, :],
                                    ones[SHIFT:SHIFT + 1, 0:1].to_broadcast([1, M])).then_inc(s_const, 1)
                dve.wait_ge(s_setup_dma, 16 * SETUP_LOADS)
                tp = [(w_t[:, :, :], slice(k * DA, (k + 1) * DA)) for k in range(3)]
                tp.append((w_p[:, :, :], slice(3 * DA, P)))
                pairs = [(raw, w_tp_hi[:, :, cols], w_tp_lo[:, :, cols]) for raw, cols in tp]
                pairs += [(w_gs[:, :, :], w_g_hi[:, :, :], w_g_lo[:, :, :]), (w_o[:, :], w_o_hi[:, :], w_o_lo[:, :])]
                for raw, hi, _lo in pairs:
                    dve.tensor_copy(hi, raw).then_inc(s_whi, 1)
                for k, (raw, hi, lo) in enumerate(pairs):
                    dve.wait_ge(s_whi, k + 1)
                    dve.tensor_tensor(lo, raw, hi.bitcast(F32), ALU.subtract).then_inc(s_wlo, 1)

                for t in range(2):
                    dve.wait_ge(s_first_hi, t + 1)
                    dve.tensor_tensor(x_lo[:, t, :, :], x_raw[:, t, :, :], x_hi[:, t, :, :].bitcast(F32),
                                      ALU.subtract).then_inc(s_first_lo, 1)

            @block.scalar
            def _(act):
                act.wait_ge(s_first, 32)
                for t in range(2):
                    act.copy(x_hi[:, t, :, :], x_raw[:, t, :, :]).then_inc(s_first_hi, 1)

        def is_split(q):
            return q % 2 == 1

        def pool_takes(q):
            return q % 4 == 3

        def splits(q):
            return sum(is_split(k) for k in range(q))

        def split_before(q, n):
            earlier = [k for k in range(q) if is_split(k)]
            return earlier[-n] if len(earlier) >= n else None

        def dve_los(q):
            return sum(is_split(k) and not pool_takes(k) for k in range(q))

        def pool_los(q):
            return sum(pool_takes(k) for k in range(q))

        def moments_of(pe, acc, slot, first):
            for j in range(NC):
                y2 = y_split[:, slot, j, :]
                flags = dict(start=(first and j == 0), stop=(not first and j == NC - 1))
                pe.matmul(acc[:, 0:NT], y2[:, 0:P], y2, **flags)
                last = pe.matmul(acc[:, NT:NT + UPPER], y2[:, P:2 * P], y2[:, P:], **flags)
            return last

        def image_items():
            items = [(s, "chunk") for s in CHUNK_STEPS] + [(s, "project") for s in PROJ_STEPS]
            items += [(s, "moments") for s in MOMENT_STEPS] + [(TURN_STEP, "turn_g")]
            assert len(dict(items)) == len(items)
            return sorted(items)

        def numbered(steps_and_kinds):
            seen, out = {}, []
            for step, kind in steps_and_kinds:
                out.append((step, kind, seen.get(kind, 0)))
                seen[kind] = seen.get(kind, 0) + 1
            return out

        def stream(img, opening=False, closing=False):
            if opening:
                PROJ0, CHUNK0, ROW0 = 0, 0, 0
                items = numbered([(None, "project")] * TILES + [(None, "turn_g")] + [(None, "chunk")] * LEAD)
            else:
                PROJ0, CHUNK0, ROW0 = TILES, LEAD, 2
                items = [(u * STEPS + step, kind) for u in range(GROUP) for step, kind in image_items()]
                if closing:
                    items = [(step, kind) for step, kind in items
                             if kind not in ("project", "turn_g") or step < (GROUP - 1) * STEPS]
                    chunks = [item for item in items if item[1] == "chunk"]
                    items = [item for item in items if item not in chunks[GROUP * CHUNKS - LEAD:]]
                items = numbered(items)
            at_step = {step: (n, kind, k) for n, (step, kind, k) in enumerate(items)}
            tiles = GROUP * TILES
            PROJECTED = sum(kind == "project" for _step, kind, _k in items)
            last_q = tiles * MB
            loads = GROUP * TILES - TILES if closing else PROJECTED + 2
            rows = tiles if closing else tiles + 2

            def half_of(kind, k):
                n = [(x, y) for _s, x, y in items].index((kind, k))
                return ps_scores[:, n % 2, :]

            def out_bank(t, half):
                return (t + half) % 2 if t == tiles - 1 else t % 2

            def which(k):
                return (PROJ0 + k) // TILES % 2, (PROJ0 + k) % TILES

            with nc.Block() as block:
                @block.sync
                def _(sp):
                    def load_xt(k):
                        if k >= 4:
                            sp.wait_ge(s_xhi, k - 3)
                            sp.wait_ge(s_xlo, k - 3)
                        ahead, place = divmod(PROJ0 + k, TILES)
                        src = xT[img + ahead]
                        sp.dma_start(x_raw[:, k % 2, :, :], src[place]).then_inc(s_xt[k % 2], 16)

                    def load_xn(t):
                        if t >= 3:
                            sp.wait_ge(s_y, 2 * (t - 2))
                        sp.dma_start(x_nat[:, t % 3, :, :], xN[img * TILES + t]).then_inc(s_xn[t % 3], 16)

                    def store_y(t):
                        sp.wait_ge(s_y, 2 * (t + 1))
                        sp.dma_start(yN[img * TILES + t], y_val[:, t % 3, :, :]).then_inc(s_yst[t % 3], 16)

                    load_xt(2)
                    load_xt(3)
                    if opening:
                        for k in range(4, TILES + 2):
                            load_xt(k)
                        return
                    for t in range(3):
                        load_xn(t)
                    for q in range(last_q):
                        t, b = divmod(q, MB)
                        _n, kind, k = at_step.get(q - 4, (None, None, None))
                        if kind == "project" and k + 4 < loads:
                            load_xt(k + 4)
                        if b == 5 and t >= 1:
                            store_y(t - 1)
                            if t + 2 < tiles:
                                load_xn(t + 2)
                    last = tiles - 1
                    for half in range(2):
                        sp.wait_ge(s_y, 2 * last + half + 1)
                        rows_of = slice(half * NC // 2, (half + 1) * NC // 2)
                        sp.dma_start(yN[img * TILES + last][:, rows_of, :],
                                     y_val[:, last % 3, rows_of, :]).then_inc(s_yst[last % 3], 16)
                    for k in range(3):
                        sp.wait_ge(s_yst[k], 16 * (len(range(k, tiles, 3)) + (k == last % 3)))

                @block.tensor
                def _(pe):
                    def half_free(n):
                        if n < 2:
                            return
                        _step, kind, k = items[n - 2]
                        if kind == "chunk":
                            pe.wait_ge(s_z, k + 1)
                        elif kind == "project":
                            pe.wait_ge(s_th_lo, k + 1)
                            pe.wait_ge(s_gpool, k + 1)
                        elif kind == "moments":
                            pe.wait_ge(s_momadd, k + 1)
                        else:
                            pe.wait_ge(s_gval, k + 1)

                    def project(acc2, k):
                        slot = k % 2
                        acc = acc2[:, 0:NT]
                        if k >= 2:
                            pe.wait_ge(s_xhi, k - 1)
                        for cc in range(CC):
                            pe.matmul(acc, w_tp_hi[:, cc, :], x_hi[:, slot, cc, :], start=(cc == 0), stop=False)
                            pe.matmul(acc, w_tp_lo[:, cc, :], x_hi[:, slot, cc, :], start=False, stop=False)
                        if k >= 2:
                            pe.wait_ge(s_xlo, k - 1)
                        for cc in range(CC):
                            last = pe.matmul(acc, w_tp_hi[:, cc, :], x_lo[:, slot, cc, :],
                                             start=False, stop=(cc == CC - 1))
                        last.then_inc(s_tp, 1)

                    def project_g(acc2, k):
                        slot = k % 2
                        acc = acc2[:, NT:2 * NT]
                        for cc in range(CC):
                            pe.matmul(acc, w_g_hi[:, cc, :], x_hi[:, slot, cc, :], start=(cc == 0), stop=False)
                            pe.matmul(acc, w_g_lo[:, cc, :], x_hi[:, slot, cc, :], start=False, stop=False)
                            last = pe.matmul(acc, w_g_hi[:, cc, :], x_lo[:, slot, cc, :],
                                             start=False, stop=(cc == CC - 1))
                        last.then_inc(s_g, 1)

                    def turn_g(acc, k):
                        pe.wait_ge(s_gpool, TILES * (k + 1))
                        for m in range(MB):
                            last = pe.transpose(acc[:, m * P:(m + 1) * P], g_pool[:, m, :], ident[:, :])
                        last.then_inc(s_gT, 1)

                    def scores(acc, k):
                        c = CHUNK0 + k
                        image, c_in = divmod(c, CHUNKS)
                        if c_in == 0:
                            done = TILES * (1 if opening else image)
                            pe.wait_ge(s_phi, 2 * done)
                            pe.wait_ge(s_philo, done)
                            pe.wait_ge(s_th_lo, done)
                        for h in range(2):
                            last = pe.matmul(acc[:, h * NT:(h + 1) * NT],
                                             theta[0:SHIFT, image % 2, c_in * P:(c_in + 1) * P],
                                             phi[0:SHIFT, image % 2, h * NT:(h + 1) * NT], start=True, stop=True)
                        last.then_inc(s_scores, 1)

                    def moments(acc, k):
                        t = 2 * (k - 1)
                        if k >= 1:
                            pe.wait_ge(s_yhi, t + 2)
                            pe.wait_ge(s_ylo, t + 2)
                        moments_of(pe, acc, t % Y_RING, True)

                    def moments_rest(acc, k):
                        t = 2 * (k - 1)
                        moments_of(pe, acc, (t + 1) % Y_RING, False).then_inc(s_mom, 1)

                    def item(n):
                        _step, kind, k = items[n]
                        half_free(n)
                        work = {"chunk": scores, "project": project, "moments": moments, "turn_g": turn_g}[kind]
                        work(ps_scores[:, n % 2, :], k)

                    def item_rest(n):
                        _step, kind, k = items[n]
                        if kind == "project":
                            project_g(ps_scores[:, n % 2, :], k)
                        elif kind == "moments":
                            moments_rest(ps_scores[:, n % 2, :], k)

                    def turn_max(t):
                        if NC * (t + 1) > CHUNK0:
                            pe.wait_ge(s_max, NC * (t + 1) - CHUNK0)
                        if t >= 3:
                            pe.wait_ge(s_y, 2 * (t - 2))
                        for j in range(NC):
                            last = pe.transpose(ps_oy[0:1, (t + 1) % 2, j * P:(j + 1) * P].bitcast(F32R),
                                                neg_max[:, t % TURNS, j:j + 1], ident_r[:, :])
                        last.then_inc(s_rowT, 1)

                    def scores_t(q):
                        t, b = divmod(q, MB)
                        if b == 0 and t >= 2:
                            pe.wait_ge(s_row, t - 1)
                        if q >= 2:
                            pe.wait_ge(s_e, q - 1)
                        u, place = t // TILES % 2, t % TILES
                        pe.matmul(ps_st[:, q % 2, :], phi[0:SHIFT + 1, u, b * P:(b + 1) * P],
                                  theta[0:SHIFT + 1, u, place * NT:(place + 1) * NT],
                                  start=True, stop=True).then_inc(s_st, 1)

                    def attend(q):
                        t, b = divmod(q, MB)
                        u = t // TILES % 2
                        acc = ps_oy[:, t % 2, :]
                        if b == 0 and t >= 1:
                            if t >= 2:
                                pe.wait_ge(s_y, 2 * (t - 1))
                            pe.wait_ge(s_row, min(t, rows - 2))
                        if b == 0 and t % TILES == 0 and t >= TILES:
                            pe.wait_ge(s_glo, t // TILES)
                        first, last = b == 0, b == MB - 1
                        if is_split(q):
                            e_slot = splits(q) % SPLIT_RING
                            pe.wait_ge(s_ehi, splits(q + 1))
                            pe.matmul(acc, g_hi[:, u, b, :], e_hi[:, e_slot, :], start=first, stop=False)
                            pe.matmul(acc, g_lo[:, u, b, :], e_hi[:, e_slot, :], start=False, stop=False)
                            if pool_takes(q):
                                pe.wait_ge(s_elo_p, pool_los(q + 1))
                            else:
                                pe.wait_ge(s_elo_v, dve_los(q + 1))
                            pe.matmul(acc, g_hi[:, u, b, :], e_lo[:, e_slot, :], start=False,
                                      stop=last).then_inc(s_av, 1)
                        else:
                            pe.wait_ge(s_e, q + 1)
                            pe.matmul(acc, g_val[:, u, b, :], e_val[:, q % RING, :], start=first,
                                      stop=last).then_inc(s_av, 1)

                    def project_out(t, half):
                        if half == 0:
                            pe.wait_ge(s_olo, t + 1)
                        elif t < tiles - 1:
                            pe.wait_ge(s_y, 2 * t + 1)
                        else:
                            pe.wait_ge(s_y, 2 * t)
                            pe.wait_ge(s_row, rows - 2)
                        for k in range(2):
                            cols = slice((2 * half + k) * P, (2 * half + k + 1) * P)
                            acc = ps_oy[:, out_bank(t, half), k * C:(k + 1) * C]
                            pe.matmul(acc, o_hi[:, t % 2, cols], w_o_hi[:, :], start=True, stop=False)
                            pe.matmul(acc, o_hi[:, t % 2, cols], w_o_lo[:, :], start=False, stop=False)
                            last = pe.matmul(acc, o_lo[:, t % 2, cols], w_o_hi[:, :], start=False, stop=True)
                        last.then_inc(s_yps, 1)

                    if opening:
                        for n in range(len(items)):
                            item(n)
                            item_rest(n)
                        turn_max(0)
                        turn_max(1)
                        return
                    for q in range(AHEAD):
                        scores_t(q)
                        if q == 1:
                            item(0)
                    for q in range(last_q):
                        t, b = divmod(q, MB)
                        if q + AHEAD < last_q:
                            scores_t(q + AHEAD)
                        if b in (2, 4) and t >= 1:
                            project_out(t - 1, b // 4)
                        attend(q)
                        if q in at_step and q > 0:
                            item(at_step[q][0])
                            item_rest(at_step[q][0])
                        if b == 6 and t + 2 < rows:
                            turn_max(t + 2)
                    project_out(tiles - 1, 0)
                    project_out(tiles - 1, 1)

                @block.scalar
                def _(act):
                    def split_x(k):
                        act.wait_ge(s_xt[k % 2], 16 * (k // 2))
                        act.wait_ge(s_g, k - 1)
                        act.copy(x_hi[:, k % 2, :, :], x_raw[:, k % 2, :, :]).then_inc(s_xhi, 1)

                    def theta_hi(k):
                        buf, place = which(k)
                        act.wait_ge(s_tp, k + 1)
                        act.copy(theta[0:SHIFT, buf, place * NT:(place + 1) * NT],
                                 half_of("project", k)[0:SHIFT, 0:NT]).then_inc(s_th_hi, 1)

                    def stack_phi(k):
                        buf, place = which(k)
                        cols = slice(place * P, (place + 1) * P)
                        act.wait_ge(s_phipool, k + 1)
                        if k >= 2:
                            act.wait_ge(s_philo, k - 1)
                        act.copy(phi_hi[SHIFT:, k % 2, :], phi_pool[SHIFT:, k % 2, :]).then_inc(s_phihi, 1)
                        act.wait_ge(s_phihi, k + 1)
                        for m in range(2):
                            act.copy(phi[m * DA:(m + 1) * DA, buf, cols],
                                     phi_hi[SHIFT:, k % 2, :].bitcast(F32)).then_inc(s_phi, 1)

                    def copy_g(k):
                        act.wait_ge(s_gT, k + 1)
                        act.copy(g_val[:, which(k * TILES)[0], :, :].rearrange("p m d -> p (m d)"),
                                 half_of("turn_g", k)).then_inc(s_gval, 1)

                    def exp_sum(k):
                        t, j = divmod(CHUNK0 + k, NC)
                        act.wait_ge(s_max, k + 1)
                        if k >= 2:
                            act.wait_ge(s_z, k - 1)
                        act.activation(dump[:, k % 2, :], half_of("chunk", k), ACT.Exp,
                                       bias=neg_max[:, t % TURNS, j:j + 1].bitcast(F32),
                                       accum_out=total[:, t % TURNS, j:j + 1]).then_inc(s_z, 1)

                    def copy_row(t):
                        act.wait_ge(s_rowT, t + 1 - ROW0)
                        u, place = t // TILES % 2, t % TILES
                        act.copy(theta[SHIFT:SHIFT + 1, u, place * NT:(place + 1) * NT],
                                 ps_oy[0:1, (t + 1) % 2, :]).then_inc(s_row, 1)

                    def exponentiate(q):
                        act.wait_ge(s_st, q + 1)
                        if q >= RING:
                            act.wait_ge(s_av, q - RING + 1)
                        act.activation(e_val[:, q % RING, :], ps_st[:, q % 2, :], ACT.Exp).then_inc(s_e, 1)

                    def split_o(t):
                        act.wait_ge(s_av, MB * (t + 1))
                        if t >= 2:
                            act.wait_ge(s_yps, 2 * (t - 1))
                        act.copy(o_hi[:, t % 2, :], ps_oy[:, t % 2, :]).then_inc(s_ohi, 1)

                    if opening:
                        for k in range(TILES + 1):
                            if k >= 1:
                                theta_hi(k - 1)
                                split_x(k + 1)
                            if k >= 2:
                                stack_phi(k - 2)
                        stack_phi(TILES - 1)
                        copy_g(0)
                        for k in range(LEAD):
                            exp_sum(k)
                        copy_row(0)
                        copy_row(1)
                        return
                    for q in range(AHEAD):
                        exponentiate(q)
                    for q in range(last_q):
                        t, b = divmod(q, MB)
                        if b == 0 and t >= 1:
                            split_o(t - 1)
                        if b == 7 and t + 2 < rows:
                            copy_row(t + 2)
                        if q + AHEAD < last_q:
                            exponentiate(q + AHEAD)
                        for before in (1, 2, 3):
                            _n, kind, k = at_step.get(q - before, (None, None, None))
                            if kind == "chunk" and before == 1:
                                exp_sum(k)
                            elif kind == "turn_g" and before == 1:
                                copy_g(k)
                            elif kind == "project" and before == 1:
                                theta_hi(k)
                            elif kind == "project" and before == 2 and k + 2 < loads:
                                split_x(k + 2)
                            elif kind == "project" and before == 3:
                                stack_phi(k)

                @block.vector
                def _(dve):
                    def window(ap):
                        return ap.rearrange("p (r h w v) -> p r w h v", r=ROWS // 2, h=2, v=2)

                    def pooled(ap):
                        return ap.rearrange("p (r w) -> p r w", r=ROWS // 2)

                    def pool_phi(k):
                        dve.wait_ge(s_tp, k + 1)
                        if k >= 2:
                            dve.wait_ge(s_phihi, k - 1)
                            dve.wait_ge(s_philo, k - 1)
                        dve.tensor_reduce(pooled(phi_pool[SHIFT:, k % 2, :]),
                                          window(half_of("project", k)[SHIFT:, 0:NT]),
                                          AX.XY, ALU.max).then_inc(s_phipool, 1)

                    def pool_g(k):
                        dve.wait_ge(s_g, k + 1)
                        if k >= TILES:
                            dve.wait_ge(s_gT, k // TILES)
                        dve.tensor_reduce(pooled(g_pool[:, k % TILES, :]),
                                          window(half_of("project", k)[:, NT:2 * NT]),
                                          AX.XY, ALU.max).then_inc(s_gpool, 1)

                    def theta_lo(k):
                        buf, place = which(k)
                        dve.wait_ge(s_th_hi, k + 1)
                        dst = theta[DA:2 * DA, buf, place * NT:(place + 1) * NT]
                        dve.tensor_tensor(dst, half_of("project", k)[DA:2 * DA, 0:NT],
                                          dst.bitcast(F32), ALU.subtract).then_inc(s_th_lo, 1)

                    def phi_lo(k):
                        buf, place = which(k)
                        dve.wait_ge(s_phihi, k + 1)
                        dve.tensor_tensor(phi[2 * DA:3 * DA, buf, place * P:(place + 1) * P],
                                          phi_pool[SHIFT:, k % 2, :],
                                          phi_hi[SHIFT:, k % 2, :].bitcast(F32), ALU.subtract).then_inc(s_philo, 1)

                    def split_g(k):
                        buf = which(k * TILES)[0]
                        dve.wait_ge(s_gval, k + 1)
                        dve.tensor_copy(g_hi[:, buf, :, :], g_val[:, buf, :, :]).then_inc(s_ghi, 1)
                        dve.wait_ge(s_ghi, k + 1)
                        dve.tensor_tensor(g_lo[:, buf, :, :], g_val[:, buf, :, :],
                                          g_hi[:, buf, :, :].bitcast(F32), ALU.subtract).then_inc(s_glo, 1)

                    def maximum(k):
                        t, j = divmod(CHUNK0 + k, NC)
                        dve.wait_ge(s_scores, k + 1)
                        dve.tensor_reduce(neg_max[:, t % TURNS, j:j + 1], half_of("chunk", k), AX.X, ALU.max,
                                          negate=True).then_inc(s_max, 1)

                    def add_moments(k):
                        dve.wait_ge(s_mom, k + 1)
                        if k >= 1:
                            dve.wait_ge(s_momadd, k)
                        dve.tensor_tensor(moments_flat, half_of("moments", k)[:, 0:NT + UPPER], moments_flat,
                                          ALU.add).then_inc(s_momadd, 1)

                    def split_e_hi(q):
                        dve.wait_ge(s_e, q + 1)
                        used = split_before(q, SPLIT_RING)
                        if used is not None:
                            dve.wait_ge(s_av, used + 1)
                        dve.tensor_copy(e_hi[:, splits(q) % SPLIT_RING, :], e_val[:, q % RING, :]).then_inc(s_ehi, 1)

                    def split_e_lo(q):
                        dve.wait_ge(s_ehi, splits(q + 1))
                        dve.tensor_tensor(e_lo[:, splits(q) % SPLIT_RING, :], e_val[:, q % RING, :],
                                          e_hi[:, splits(q) % SPLIT_RING, :].bitcast(F32), ALU.subtract
                                          ).then_inc(s_elo_v, 1)

                    def round_o(t):
                        dve.wait_ge(s_av, MB * (t + 1))
                        dve.wait_ge(s_yps, 2 * (t - 1))
                        dve.tensor_copy(o_hi[:, t % 2, :], ps_oy[:, t % 2, :]).then_inc(s_ohi, 1)

                    def split_o(t):
                        dve.wait_ge(s_ohi, t + 1)
                        dve.tensor_tensor(o_lo[:, t % 2, :], ps_oy[:, t % 2, :], o_hi[:, t % 2, :].bitcast(F32),
                                          ALU.subtract).then_inc(s_olo, 1)

                    def weight_scale(t):
                        if NC * (t + 1) > CHUNK0:
                            dve.wait_ge(s_z, NC * (t + 1) - CHUNK0)
                        dve.reciprocal(recip[:, t % 2, :], total[:, t % TURNS, :]).then_inc(s_recip, 1)
                        dve.wait_ge(s_recip, t + 1)
                        dve.tensor_scalar(scale[:, t % 2, :], recip[:, t % 2, :], sig[:, 0:1], None,
                                          ALU.mult).then_inc(s_scale, 1)

                    def residual(t, half):
                        if half == 0:
                            dve.wait_ge(s_scale, t + 1)
                            dve.wait_ge(s_xn[t % 3], 16 * (t // 3 + 1))
                            if t >= 3:
                                dve.wait_ge(s_yst[t % 3], 16 * (t // 3))
                                dve.wait_ge(s_ylo, t - 2)
                                dve.wait_ge(s_ysum, t - 2)
                        dve.wait_ge(s_yps, 2 * t + half + 1)
                        for k in range(2):
                            j = 2 * half + k
                            out = ps_oy[:, out_bank(t, half), k * C:(k + 1) * C]
                            last = dve.scalar_tensor_tensor(y_val[:, t % 3, j, :], out, scale[:, t % 2, j:j + 1],
                                                            x_nat[:, t % 3, j, :], ALU.mult, ALU.add)
                        last.then_inc(s_y, 1)

                    def split_y(t):
                        dve.wait_ge(s_y, 2 * (t + 1))
                        if t >= 2:
                            dve.wait_ge(s_mom, t // 2)
                        dve.tensor_copy(y_split[:, t % Y_RING, :, 0:C], y_val[:, t % 3, :, :]).then_inc(s_yhi, 1)

                    def split_y_lo(t):
                        dve.wait_ge(s_yhi, t + 1)
                        dve.wait_ge(s_ylo, t)
                        dve.tensor_tensor(y_split[:, t % Y_RING, :, C:], y_val[:, t % 3, :, :],
                                          y_split[:, t % Y_RING, :, 0:C].bitcast(F32), ALU.subtract
                                          ).then_inc(s_ylo, 1)

                    if opening:
                        for k in range(TILES + 1):
                            if k >= 1:
                                pool_phi(k - 1)
                                pool_g(k - 1)
                                theta_lo(k - 1)
                            if k >= 2:
                                phi_lo(k - 2)
                        phi_lo(TILES - 1)
                        for k in range(LEAD):
                            maximum(k)
                            if k == 1:
                                split_g(0)
                        return
                    for q in range(0, SPLIT_AHEAD):
                        if is_split(q):
                            split_e_hi(q)
                            if not pool_takes(q):
                                split_e_lo(q)
                    for q in range(last_q):
                        t, b = divmod(q, MB)
                        if b in (3, 5) and t >= 1:
                            residual(t - 1, b // 5)
                        if q + SPLIT_AHEAD < last_q and is_split(q + SPLIT_AHEAD):
                            split_e_hi(q + SPLIT_AHEAD)
                        if b == 5 and t >= 1:
                            split_y(t - 1)
                        if b == 2:
                            weight_scale(t)
                        if b == 0 and t >= 1:
                            split_o(t - 1)
                        if q + SPLIT_AHEAD < last_q and is_split(q + SPLIT_AHEAD) and not pool_takes(q + SPLIT_AHEAD):
                            split_e_lo(q + SPLIT_AHEAD)
                        for before in (1, 2, 4):
                            _n, kind, k = at_step.get(q - before, (None, None, None))
                            if kind == "chunk" and before == 1:
                                maximum(k)
                            elif kind == "moments" and before == 1:
                                add_moments(k)
                            elif kind == "turn_g" and before == 2:
                                split_g(k)
                            elif kind == "project" and before == 1:
                                pool_phi(k)
                                pool_g(k)
                                theta_lo(k)
                            elif kind == "project" and before == 4:
                                phi_lo(k)
                    round_o(tiles - 1)
                    split_o(tiles - 1)
                    residual(tiles - 1, 0)
                    residual(tiles - 1, 1)
                    split_y(tiles - 1)
                    split_y_lo(tiles - 1)

                @block.gpsimd
                def _(pool):
                    def split_x(k):
                        pool.wait_ge(s_xhi, k - 1)
                        pool.tensor_tensor(x_lo[:, k % 2, :, :], x_raw[:, k % 2, :, :],
                                           x_hi[:, k % 2, :, :].bitcast(F32), ALU.subtract).then_inc(s_xlo, 1)

                    def split_e(q):
                        pool.wait_ge(s_ehi, splits(q + 1))
                        pool.tensor_tensor(e_lo[:, splits(q) % SPLIT_RING, :], e_val[:, q % RING, :],
                                           e_hi[:, splits(q) % SPLIT_RING, :].bitcast(F32), ALU.subtract
                                           ).then_inc(s_elo_p, 1)

                    def sum_y(t):
                        pool.wait_ge(s_y, 2 * (t + 1))
                        if t >= 1:
                            pool.wait_ge(s_ysum, t)
                        pool.tensor_tensor(y_sum[:, :, :], y_sum[:, :, :], y_val[:, t % 3, :, :],
                                           ALU.add).then_inc(s_ysum, 1)

                    def split_y(t):
                        pool.wait_ge(s_yhi, t + 1)
                        pool.tensor_tensor(y_split[:, t % Y_RING, :, C:], y_val[:, t % 3, :, :],
                                           y_split[:, t % Y_RING, :, 0:C].bitcast(F32), ALU.subtract
                                           ).then_inc(s_ylo, 1)

                    if opening:
                        for k in range(2, TILES + 2):
                            split_x(k)
                        return
                    for q in range(last_q):
                        t, b = divmod(q, MB)
                        if b == 5 and t >= 1:
                            split_y(t - 1)
                        if b == 1 and t >= 2:
                            sum_y(t - 2)
                        if q + SPLIT_AHEAD < last_q and pool_takes(q + SPLIT_AHEAD):
                            split_e(q + SPLIT_AHEAD)
                        _n, kind, k = at_step.get(q - 3, (None, None, None))
                        if kind == "project" and k + 2 < loads:
                            split_x(k + 2)
                    sum_y(tiles - 2)
                    sum_y(tiles - 1)

            nc.all_engine_barrier(sems_to_clear=range(cleared[0].num, cleared[-1].num + 1))

        stream(0, opening=True)
        with nc.Fori(0, B // GROUP - 1) as group:
            stream(group * GROUP)
        stream(B - GROUP, closing=True)

        s_rest = sem("s_rest")
        with nc.Block() as block:
            @block.tensor
            def _(pe):
                moments_of(pe, ps_scores[:, 0, :], Y_RING - 2, True)
                moments_of(pe, ps_scores[:, 0, :], Y_RING - 1, False).then_inc(s_rest, 1)

            @block.vector
            def _(dve):
                dve.wait_ge(s_rest, 1)
                dve.tensor_tensor(moments_flat, ps_scores[:, 0, 0:NT + UPPER], moments_flat,
                                  ALU.add).then_inc(s_rest, 1)

        row_s = sb("row_s", [1, C])
        mean = sb("mean", [P, CC])
        scratch = e_val[:, :, :].rearrange("p r n -> p (r n)").rearrange("p (k c) -> p k c", c=P)
        hl = scratch[:, 0:3, :]
        a_mat = scratch[:, 3:6, :]
        elim = e_val[:, :, :].rearrange("p r n -> p (r n)")[:, 6 * P:8 * P]
        diag = scratch[:, 8, :]
        w_inv = scratch[:, 9:11, :]
        w_invT = scratch[:, 11:13, :]
        b_mat = scratch[:, 13, :]
        x_mat = scratch[:, 14, :]
        w_10 = scratch[:, 15, :]
        wg = scratch[:, 16:19, :]
        wgT = scratch[:, 19:22, :]
        more = x_raw[:, :, :, :].rearrange("p s a n -> p (s a n)").rearrange("p (k c) -> p k c", c=P)
        schur = more[:, 0, :]
        above = more[:, 1, :]
        product = more[:, 3, :]
        step_T = more[:, 4, :]
        off = more[:, 5, :]
        rinv = sb("rinv", [P, 1])
        mult = sb("mult", [P, 1])
        dcol = sb("dcol", [P, 3])
        settled = sb("settled", [P, 3])
        settled_rows = sb("settled_rows", [1, 1], mybir.dt.int32)
        wgT_hi = phi[:, 0, 0:3 * P].rearrange("p (k c) -> p k c", k=3)
        wgT_lo = phi[:, 1, 0:3 * P].rearrange("p (k c) -> p k c", k=3)
        bias = sb("bias", [P, CC])

        out_sb = y_val[:, 0:2, :, :].rearrange("p s j c -> p s (j c)").rearrange("p s (a n) -> p s a n", a=CC)
        y_slots = []
        for room in (theta[:, :, :].rearrange("p u n -> p (u n)"),
                     y_split[:, :, :, :].rearrange("p s j c -> p (s j c)")):
            slots = room.bitcast(F32).rearrange("p (s j c) -> p s j c", j=NC, c=C)
            y_slots += [slots[:, k, :, :] for k in range(slots.shape[1])]
        landed = [sem(f"s_landed{k}") for k in range(len(y_slots))]
        assert B * TILES % len(y_slots) == 0
        covariance(nc, sem("s_cov"), y_sum, row_s, mean, hl, a_mat, moment, ident, ones,
                   ps_scores, ps_st, ps_oy, TOTAL, y_slots, landed, yN)
        newton(nc, sem("s_newton"), a_mat, schur, above, below, ident, ones, product, step_T, off,
               dcol, settled, settled_rows, w_inv, w_invT, b_mat, x_mat, w_10, ps_scores, ps_st, ps_oy)
        nc.all_engine_barrier()
        rows = nc.values_load(settled_rows[0:1, 0:1], min_val=0, max_val=P,
                              skip_runtime_bounds_check_because="a count of partitions")
        with nc.If(rows < P):
            eliminate(nc, sem("s_elim"), a_mat, elim, diag, rinv, mult, dcol, below, ident,
                      w_inv, w_invT, b_mat, x_mat, w_10, ps_st, ps_oy)
        fold(nc, sem("s_fold"), w_inv, w_10, wg, wgT, wgT_hi, wgT_lo, gam, bet, mean, bias, ident, ps_st, ps_oy)

        whiten(nc, ctx, landed, yN, outT, y_slots, out_sb, ps_scores, ps_st, ps_oy, ident, wgT_hi, wgT_lo, bias,
               x_hi, x_lo, B * TILES, TILES)


def covariance(nc, s_f, y_sum, row_s, mean, hl, a_mat, moment, ident, ones, ps_scores, ps_st, ps_oy, total,
               y_slots, landed, yN):
    C = row_s.shape[1]
    CC = C // P
    with nc.Block() as block:
        @block.sync
        def _(sp):
            for k, slot in enumerate(y_slots):
                sp.dma_start(slot, yN[k]).then_inc(landed[k], 16)

        @block.tensor
        def _(pe):
            for j in range(NC):
                last = pe.matmul(ps_oy[0:1, 0, 0:C], ones[:, 0:1], y_sum[:, j, :], start=(j == 0), stop=(j == NC - 1))
            last.then_inc(s_f, 1)
            for a in range(CC):
                for j in range(NC):
                    last = pe.matmul(ps_oy[:, 1, a:a + 1], y_sum[:, j, a * P:(a + 1) * P], ones[:, 0:1],
                                     start=(j == 0), stop=(j == NC - 1))
            last.then_inc(s_f, 1)
            pe.wait_ge(s_f, 4)
            for a in range(CC):
                last = pe.matmul(ps_st[:, a, 0:C], row_s[0:1, a * P:(a + 1) * P], row_s[0:1, :],
                                 start=True, stop=True)
            last.then_inc(s_f, 1)
            pe.wait_ge(s_f, 8)
            for k in range(3):
                last = pe.transpose(ps_scores[:, 0, k * P:(k + 1) * P], hl[:, k, :], ident[:, :])
            last.then_inc(s_f, 1)

        @block.vector
        def _(dve):
            dve.wait_ge(s_f, 2)
            dve.tensor_copy(row_s[0:1, :], ps_oy[0:1, 0, 0:C]).then_inc(s_f, 1)
            dve.tensor_scalar(mean[:, :], ps_oy[:, 1, 0:CC], 1.0 / total, None, ALU.mult).then_inc(s_f, 1)
            dve.wait_ge(s_f, 5)
            for k, (a, col) in enumerate(((0, 2 * P), (1, P), (1, 2 * P))):
                dve.tensor_copy(hl[:, k, :], moment[:, a, col:col + P]).then_inc(s_f, 1)
            dve.wait_ge(s_f, 9)
            blocks = ((moment[:, 0, 0:P], hl[:, 0, :], ps_st[:, 0, 0:P]),
                      (moment[:, 0, P:2 * P], moment[:, 0, 3 * P:4 * P], ps_st[:, 0, P:2 * P]),
                      (moment[:, 1, 0:P], hl[:, 2, :], ps_st[:, 1, P:2 * P]))
            n = 9
            for k, (hh, own, outer) in enumerate(blocks):
                dst = a_mat[:, k, :]
                dve.tensor_copy(dst, hh).then_inc(s_f, 1)
                dve.wait_ge(s_f, n + 1)
                dve.tensor_tensor(dst, own, dst, ALU.add).then_inc(s_f, 1)
                dve.wait_ge(s_f, n + 2)
                dve.tensor_tensor(dst, ps_scores[:, 0, k * P:(k + 1) * P], dst, ALU.add).then_inc(s_f, 1)
                dve.wait_ge(s_f, n + 3)
                dve.scalar_tensor_tensor(dst, outer, -1.0 / total, dst, ALU.mult, ALU.add).then_inc(s_f, 1)
                dve.wait_ge(s_f, n + 4)
                dve.tensor_scalar(dst, dst, (1.0 - WHITEN_EPS) / (total - 1.0), None, ALU.mult).then_inc(s_f, 1)
                n += 5
                if k != 1:
                    dve.wait_ge(s_f, n)
                    dve.scalar_tensor_tensor(dst, ident[:, :], WHITEN_EPS, dst, ALU.mult, ALU.add).then_inc(s_f, 1)
                    n += 1


def newton(nc, s_f, a_mat, schur, above, below, ident, ones, product, step_T, off, dcol, settled,
           settled_rows, w_inv, w_invT, b_mat, x_mat, w_10, ps_scores, ps_st, ps_oy):
    MASK, START, TURN, CHECK, BETWEEN = 2, 6, 7, 4, 5
    first = (MASK, MASK + START + TURN * NEWTON_STEPS + CHECK + BETWEEN)
    checked = [f + START + TURN * NEWTON_STEPS + CHECK for f in first]

    with nc.Block() as block:
        @block.tensor
        def _(pe):
            def after(n):
                pe.wait_ge(s_f, n)

            pe.transpose(ps_oy[:, 0, 0:P], below[:, :], ident[:, :]).then_inc(s_f, 1)
            for half in range(2):
                a = a_mat[:, 0, :] if half == 0 else schur
                w, wT = w_inv[:, half, :], w_invT[:, half, :]
                for i in range(NEWTON_STEPS):
                    base = first[half] + START + TURN * i
                    after(base)
                    pe.matmul(ps_st[:, 0, 0:P], a, wT, start=True, stop=True).then_inc(s_f, 1)
                    after(base + 2)
                    pe.matmul(ps_st[:, 1, 0:P], wT, product, start=True, stop=True).then_inc(s_f, 1)
                    after(base + 4)
                    pe.matmul(ps_oy[:, 0, 0:P], step_T, w, start=True, stop=True)
                    pe.matmul(ps_oy[:, 1, 0:P], w, step_T, start=True, stop=True).then_inc(s_f, 1)
                after(checked[half])
                if half == 0:
                    pe.matmul(ps_scores[:, 0, 0:P], wT, a_mat[:, 1, :], start=True, stop=True).then_inc(s_f, 1)
                    after(checked[0] + 2)
                    pe.matmul(ps_scores[:, 1, 0:P], b_mat[:, :], b_mat[:, :], start=True, stop=True)
                    pe.matmul(ps_scores[:, 1, P:2 * P], b_mat[:, :], w, start=True,
                              stop=True).then_inc(s_f, 1)
                else:
                    pe.matmul(ps_scores[:, 0, 0:P], wT, x_mat[:, :], start=True, stop=True)
                    pe.matmul(ps_scores[0:1, 1, 0:1], settled[:, 2:3], ones[:, 0:1], start=True,
                              stop=True).then_inc(s_f, 1)

        @block.vector
        def _(dve):
            n = [1]

            def step(ins):
                ins.then_inc(s_f, 1)
                n[0] += 1

            def others(count=1):
                n[0] += count

            def now():
                dve.wait_ge(s_f, n[0])

            now()
            step(dve.scalar_tensor_tensor(above, ident[:, :], -0.5, ps_oy[:, 0, 0:P], ALU.mult, ALU.add))
            for half in range(2):
                a = a_mat[:, 0, :] if half == 0 else schur
                w, wT = w_inv[:, half, :], w_invT[:, half, :]
                assert n[0] == first[half]
                step(dve.tensor_tensor(off, a, ident[:, :], ALU.mult))
                now()
                step(dve.tensor_reduce(dcol[:, 0:1], off, AX.X, ALU.add))
                now()
                step(dve.reciprocal(dcol[:, 1:2], dcol[:, 0:1]))
                others()
                now()
                step(dve.tensor_scalar(w, ident[:, :], dcol[:, 2:3], None, ALU.mult))
                step(dve.tensor_scalar(wT, ident[:, :], dcol[:, 2:3], None, ALU.mult))
                for i in range(NEWTON_STEPS):
                    assert n[0] == first[half] + START + TURN * i
                    others()
                    now()
                    step(dve.tensor_copy(product, ps_st[:, 0, 0:P]))
                    others()
                    now()
                    step(dve.tensor_tensor(step_T, ps_st[:, 1, 0:P], above, ALU.mult))
                    others()
                    now()
                    step(dve.scalar_tensor_tensor(w, w, 1.5, ps_oy[:, 0, 0:P], ALU.mult, ALU.add))
                    step(dve.scalar_tensor_tensor(wT, wT, 1.5, ps_oy[:, 1, 0:P], ALU.mult, ALU.add))
                step(dve.tensor_tensor(off, ps_st[:, 1, 0:P], ident[:, :], ALU.subtract))
                now()
                step(dve.tensor_tensor(off, off, off, ALU.mult))
                now()
                step(dve.tensor_reduce(dcol[:, 0:1], off, AX.X, ALU.add))
                now()
                if half == 0:
                    step(dve.tensor_scalar(settled[:, 0:1], dcol[:, 0:1], SETTLED, None, ALU.is_le))
                    assert n[0] == checked[0]
                    others()
                    now()
                    step(dve.tensor_copy(b_mat[:, :], ps_scores[:, 0, 0:P]))
                    others()
                    now()
                    step(dve.tensor_copy(x_mat[:, :], ps_scores[:, 1, P:2 * P]))
                    step(dve.scalar_tensor_tensor(schur, ps_scores[:, 1, 0:P], -1.0, a_mat[:, 2, :],
                                                  ALU.mult, ALU.add))
                    now()
                else:
                    step(dve.scalar_tensor_tensor(settled[:, 2:3], dcol[:, 0:1], SETTLED, settled[:, 0:1],
                                                  ALU.is_le, ALU.mult))
                    assert n[0] == checked[1]
                    others()
                    now()
                    step(dve.tensor_scalar(w_10[:, :], ps_scores[:, 0, 0:P], -1.0, None, ALU.mult))
                    step(dve.tensor_copy(settled_rows[0:1, 0:1], ps_scores[0:1, 1, 0:1]))

        @block.scalar
        def _(act):
            for half in range(2):
                act.wait_ge(s_f, first[half] + 3)
                act.activation(dcol[:, 2:3], dcol[:, 1:2], ACT.Sqrt).then_inc(s_f, 1)


def eliminate(nc, s_f, a_mat, elim, diag, rinv, mult, dcol, below, ident, w_inv, w_invT, b_mat, x_mat, w_10,
              ps_st, ps_oy):
    PIVOT, ROOT, BETWEEN = 4, 5, 7
    first = (0, 2 + PIVOT * P + ROOT + BETWEEN)
    rooted = [f + 2 + PIVOT * P + ROOT for f in first]

    with nc.Block() as block:
        @block.tensor
        def _(pe):
            def after(n):
                pe.wait_ge(s_f, n)

            for half in range(2):
                for k in range(P):
                    after(first[half] + 2 + PIVOT * k)
                    pe.matmul(ps_st[:, k % 2, 0:P + 1], ident[:, k:k + 1].to_broadcast([P, P]),
                              elim[:, k:k + P + 1], start=True, stop=True).then_inc(s_f, 1)
                after(rooted[half])
                pe.transpose(ps_oy[:, 0, 0:P], w_inv[:, half, :], ident[:, :]).then_inc(s_f, 1)
                after(rooted[half] + 2)
                if half == 0:
                    pe.matmul(ps_oy[:, 0, P:2 * P], w_invT[:, 0, :], a_mat[:, 1, :], start=True,
                              stop=True).then_inc(s_f, 1)
                    after(rooted[0] + 4)
                    pe.matmul(ps_oy[:, 1, 0:P], b_mat[:, :], b_mat[:, :], start=True, stop=True)
                    pe.matmul(ps_oy[:, 1, P:2 * P], b_mat[:, :], w_inv[:, 0, :], start=True,
                              stop=True).then_inc(s_f, 1)
                else:
                    pe.matmul(ps_oy[:, 0, P:2 * P], w_invT[:, 1, :], x_mat[:, :], start=True,
                              stop=True).then_inc(s_f, 1)

        @block.vector
        def _(dve):
            n = [0]

            def step(ins):
                ins.then_inc(s_f, 1)
                n[0] += 1

            def now():
                dve.wait_ge(s_f, n[0])

            def other():
                n[0] += 1
                now()

            for half in range(2):
                src = a_mat[:, 0, :] if half == 0 else a_mat[:, 2, :]
                assert n[0] == first[half]
                step(dve.tensor_copy(elim[:, 0:P], src))
                step(dve.tensor_copy(elim[:, P:], ident[:, :]))
                for k in range(P):
                    other()
                    row = ps_st[:, k % 2, 0:P + 1]
                    step(dve.reciprocal(rinv[:, :], row[:, 0:1]))
                    now()
                    step(dve.scalar_tensor_tensor(mult[:, :], elim[:, k:k + 1], below[:, k:k + 1], rinv[:, :],
                                                  ALU.mult, ALU.mult))
                    now()
                    cols = elim[:, k:k + P + 1]
                    step(dve.scalar_tensor_tensor(cols, row, mult[:, 0:1], cols, ALU.mult, ALU.add))
                now()
                step(dve.tensor_tensor(diag[:, :], elim[:, 0:P], ident[:, :], ALU.mult))
                now()
                step(dve.tensor_reduce(dcol[:, 0:1], diag[:, :], AX.X, ALU.add))
                now()
                step(dve.reciprocal(dcol[:, 1:2], dcol[:, 0:1]))
                other()
                step(dve.tensor_scalar(w_inv[:, half, :], elim[:, P:], mult[:, 0:1], None, ALU.mult))
                assert n[0] == rooted[half]
                other()
                step(dve.tensor_copy(w_invT[:, half, :], ps_oy[:, 0, 0:P]))
                other()
                if half == 0:
                    step(dve.tensor_copy(b_mat[:, :], ps_oy[:, 0, P:2 * P]))
                    other()
                    step(dve.tensor_copy(x_mat[:, :], ps_oy[:, 1, P:2 * P]))
                    step(dve.scalar_tensor_tensor(a_mat[:, 2, :], ps_oy[:, 1, 0:P], -1.0, a_mat[:, 2, :],
                                                  ALU.mult, ALU.add))
                    now()
                else:
                    step(dve.tensor_scalar(w_10[:, :], ps_oy[:, 0, P:2 * P], -1.0, None, ALU.mult))

        @block.scalar
        def _(act):
            for half in range(2):
                act.wait_ge(s_f, rooted[half] - 2)
                act.activation(mult[:, :], dcol[:, 1:2], ACT.Sqrt).then_inc(s_f, 1)

        @block.sync
        def _(sp):
            sp.wait_ge(s_f, rooted[1])

        @block.gpsimd
        def _(pool):
            pool.wait_ge(s_f, rooted[1])


def fold(nc, s_f, w_inv, w_10, wg, wgT, wgT_hi, wgT_lo, gam, bet, mean, bias, ident, ps_st, ps_oy):
    with nc.Block() as block:
        @block.vector
        def _(dve):
            dve.tensor_scalar(wg[:, 0, :], w_inv[:, 0, :], gam[:, 0:1], None, ALU.mult).then_inc(s_f, 1)
            dve.tensor_scalar(wg[:, 1, :], w_10[:, :], gam[:, 1:2], None, ALU.mult).then_inc(s_f, 1)
            dve.tensor_scalar(wg[:, 2, :], w_inv[:, 1, :], gam[:, 1:2], None, ALU.mult).then_inc(s_f, 1)
            dve.wait_ge(s_f, 4)
            dve.tensor_copy(wgT[:, :, :], ps_st[:, 0, 0:3 * P].rearrange("p (k c) -> p k c", k=3)).then_inc(s_f, 1)
            dve.wait_ge(s_f, 5)
            dve.tensor_copy(wgT_hi[:, :, :], wgT[:, :, :]).then_inc(s_f, 1)
            dve.wait_ge(s_f, 6)
            dve.tensor_tensor(wgT_lo[:, :, :], wgT[:, :, :], wgT_hi[:, :, :].bitcast(F32), ALU.subtract
                              ).then_inc(s_f, 1)
            dve.wait_ge(s_f, 8)
            dve.scalar_tensor_tensor(bias[:, :], ps_oy[:, 1, 0:2], -1.0, bet[:, :], ALU.mult, ALU.add
                                     ).then_inc(s_f, 1)

        @block.tensor
        def _(pe):
            pe.wait_ge(s_f, 3)
            for k in range(3):
                last = pe.transpose(ps_st[:, 0, k * P:(k + 1) * P], wg[:, k, :], ident[:, :])
            last.then_inc(s_f, 1)
            pe.wait_ge(s_f, 7)
            pe.matmul(ps_oy[:, 1, 0:1], wgT[:, 0, :], mean[:, 0:1], start=True, stop=True)
            pe.matmul(ps_oy[:, 1, 1:2], wgT[:, 1, :], mean[:, 0:1], start=True, stop=False)
            pe.matmul(ps_oy[:, 1, 1:2], wgT[:, 2, :], mean[:, 1:2], start=False, stop=True).then_inc(s_f, 1)


def whiten(nc, ctx, landed, yN, outT, y_slots, out_sb, ps_scores, ps_st, ps_oy, ident, w_hi, w_lo, bias,
           yT_hi, yT_lo, tiles, per_image):
    SLOTS = len(y_slots)

    def sem(name):
        return ctx.enter_context(nc.semaphore(name))

    s_turn = sem("w_turn")
    s_hi, s_lo = sem("w_hi"), sem("w_lo")
    s_mm = sem("w_mm")
    s_outa, s_outv = sem("w_outa"), sem("w_outv")
    s_st = [sem("w_st0"), sem("w_st1")]
    turned = [ps_scores[:, k, :].rearrange("p (a n) -> p a n", a=2) for k in range(2)]
    prod = ((ps_st[:, 0, :], ps_st[:, 1, :]), (ps_oy[:, 0, :], ps_oy[:, 1, :]))

    def rounds(eng, body):
        body(0, True)
        if tiles > SLOTS:
            with eng.Fori(1, tiles // SLOTS) as n:
                body(n, False)

    with nc.Block() as block:
        @block.sync
        def _(sp):
            if tiles > SLOTS:
                with sp.Fori(1, tiles // SLOTS) as n:
                    for k in range(SLOTS):
                        sp.wait_ge(s_turn, (n - 1) * SLOTS + k + 1)
                        sp.dma_start(y_slots[k], yN[n * SLOTS + k]).then_inc(landed[k], 16)

        @block.gpsimd
        def _(pool):
            with pool.Fori(0, tiles // per_image) as img:
                for k in range(per_image):
                    pool.wait_ge(s_outa, img * per_image + k + 1)
                    pool.wait_ge(s_outv, img * per_image + k + 1)
                    pool.dma_start(outT[img, k], out_sb[:, k % 2, :, :]).then_inc(s_st[k % 2], 16)
            for slot in range(2):
                pool.wait_ge(s_st[slot], 16 * (tiles // 2))

        @block.tensor
        def _(pe):
            def turn(n, k):
                pe.wait_ge(landed[k], n * 16 + 16)
                for a in range(2):
                    for j in range(NC):
                        last = pe.transpose(turned[k % 2][:, a, j * P:(j + 1) * P],
                                            y_slots[k][:, j, a * P:(a + 1) * P], ident[:, :])
                last.then_inc(s_turn, 1)

            def product(n, k, first):
                slot = k % 2
                if not (first and k < 2):
                    pe.wait_ge(s_outa, n * SLOTS + k - 1)
                    pe.wait_ge(s_outv, n * SLOTS + k - 1)
                pe.wait_ge(s_lo, n * SLOTS + k + 1)
                blocks = (((0, 0),), ((1, 0), (2, 1)))
                for a in range(2):
                    dst = prod[slot][a]
                    for m, (w, h) in enumerate(blocks[a]):
                        hi, lo = yT_hi[:, slot, h, :], yT_lo[:, slot, h, :]
                        pe.matmul(dst, w_hi[:, w, :], hi, start=(m == 0), stop=False)
                        pe.matmul(dst, w_hi[:, w, :], lo, start=False, stop=False)
                        last = pe.matmul(dst, w_lo[:, w, :], hi, start=False, stop=(m == len(blocks[a]) - 1))
                last.then_inc(s_mm, 1)

            def body(n, first):
                for k in range(SLOTS):
                    turn(n, k)
                    if not (first and k == 0):
                        product(n, k - 1, first)

            rounds(pe, body)
            product(tiles // SLOTS - 1, SLOTS - 1, False)

        @block.scalar
        def _(act):
            def split(n, k, first):
                act.wait_ge(s_turn, n * SLOTS + k + 1)
                if not (first and k < 2):
                    act.wait_ge(s_mm, n * SLOTS + k - 1)
                act.copy(yT_hi[:, k % 2, :, :], turned[k % 2]).then_inc(s_hi, 1)

            def finish(n, k, first):
                act.wait_ge(s_mm, n * SLOTS + k + 1)
                if not (first and k < 2):
                    act.wait_ge(s_st[k % 2], n * (8 * SLOTS) + 8 * (k - k % 2))
                act.activation(out_sb[:, k % 2, 0, :], prod[k % 2][0], ACT.Identity,
                               bias=bias[:, 0:1]).then_inc(s_outa, 1)

            def body(n, first):
                for k in range(SLOTS):
                    split(n, k, first)
                    if not (first and k == 0):
                        finish(n, k - 1, first)

            rounds(act, body)
            finish(tiles // SLOTS - 1, SLOTS - 1, False)

        @block.vector
        def _(dve):
            def split(n, k, first):
                dve.wait_ge(s_hi, n * SLOTS + k + 1)
                if not (first and k < 2):
                    dve.wait_ge(s_mm, n * SLOTS + k - 1)
                dve.tensor_tensor(yT_lo[:, k % 2, :, :], turned[k % 2], yT_hi[:, k % 2, :, :].bitcast(F32),
                                  ALU.subtract).then_inc(s_lo, 1)

            def finish(n, k, first):
                dve.wait_ge(s_mm, n * SLOTS + k + 1)
                if not (first and k < 2):
                    dve.wait_ge(s_st[k % 2], n * (8 * SLOTS) + 8 * (k - k % 2))
                dve.tensor_scalar(out_sb[:, k % 2, 1, :], prod[k % 2][1], bias[:, 1:2], None,
                                  ALU.add).then_inc(s_outv, 1)

            def body(n, first):
                for k in range(SLOTS):
                    split(n, k, first)
                    if not (first and k == 0):
                        finish(n, k - 1, first)

            rounds(dve, body)
            finish(tiles // SLOTS - 1, SLOTS - 1, False)


def kernel(**inputs):
    import numpy as np
    import concourse.bacc as bacc
    from concourse.bass_utils import run_bass_kernel_spmd

    x = np.asarray(inputs["x"])
    B, H, W, C = x.shape
    N = H * W
    TILES, CC = N // NT, C // P
    flat = x.reshape(B, N, C)
    arrays = {
        "xT": np.ascontiguousarray(flat.reshape(B, TILES, NT, CC, P).transpose(0, 1, 4, 3, 2)),
        "xN": np.ascontiguousarray(flat.reshape(B * TILES, NT // P, P, C).transpose(0, 2, 1, 3)),
        "w_theta": np.asarray(inputs["L0_conv_w_theta"]),
        "w_phi": np.asarray(inputs["L0_conv_w_phi"]),
        "w_g": np.asarray(inputs["L0_conv_w_g"]),
        "w_out": np.asarray(inputs["L0_conv_w_out"]),
        "sigma": np.asarray(inputs["L0_conv_sigma"]).reshape(1),
        "gamma": np.asarray(inputs["L1_conv_gamma"]),
        "beta": np.asarray(inputs["L1_conv_beta"]),
    }
    nc = bacc.Bacc("TRN2", target_bir_lowering=False, num_devices=1)
    args = [nc.dram_tensor(f"in_{k}", a.shape, mybir.dt.from_np(a.dtype), kind="ExternalInput").ap()
            for k, a in arrays.items()]
    outT = nc.dram_tensor("out", [B, TILES, P, CC, NT], F32, kind="ExternalOutput").ap()
    attention_whitening_kernel(nc, *args, outT)
    r = run_bass_kernel_spmd(nc, [{f"in_{k}": a for k, a in arrays.items()}], core_ids=[0])
    got = r.results[0]["out"]
    return np.ascontiguousarray(got.reshape(B, TILES, P, CC, NT).transpose(0, 1, 4, 3, 2)).reshape(B, H, W, C)
```
